# Optimizing a Trainium2 kernel written in Bass

```python
import numpy as np
import jax
import jax.numpy as jnp

def _softmax(x, axis=-1):
    return jax.nn.softmax(x, axis=axis)

def _gelu(x):
    return jax.nn.gelu(x, approximate=True)

def _silu(x):
    return jax.nn.silu(x)

def _sigmoid(x):
    return jax.nn.sigmoid(x)

def _layernorm(x, axis=-1, eps=1e-05):
    m = jnp.mean(x, axis=axis, keepdims=True)
    v = jnp.var(x, axis=axis, keepdims=True)
    return (x - m) / jnp.sqrt(v + eps)

def _scatter_add(tgt, idx, src, axis=0):
    return tgt.at[idx].add(src)

def _segment_sum(src, seg, n):
    return jax.ops.segment_sum(src, seg, n)
kernel_name = 'mk_macaron_d1_jaxref_r8_dacf1b'

def setup_inputs(seed: int=0):
    np.random.seed(seed)
    _w = jnp.asarray

    def _L0_attn_setup():
        import jax, jax.numpy as jnp
        import numpy as np
        D_MODEL = 128
        NUM_HEADS = 16
        SEG = 64
        DIL = 4
        HEAD_DIM = D_MODEL // NUM_HEADS
        key = jax.random.key(seed)
        ks = jax.random.split(key, 5)
        B, S = (4, 512)
        sc = D_MODEL ** (-0.5)

        def w(k):
            return jax.random.normal(k, (D_MODEL, D_MODEL), jnp.float32) * sc
        z = jnp.zeros((D_MODEL,), jnp.float32)
        return {'x': jax.random.normal(ks[0], (B, S, D_MODEL), jnp.float32), 'Wq': w(ks[1]), 'bq': z, 'Wk': w(ks[2]), 'bk': z, 'Wv': w(ks[3]), 'bv': z, 'Wo': w(ks[4]), 'bo': z}
    _L0_attn_in = _L0_attn_setup()

    def _L0_ffn_setup():
        import jax, jax.numpy as jnp
        import numpy as np
        DIM, HEADS, EXPERTS, DFF = (128, 16, 8, 512)
        EPS = 1e-05

        def layernorm(x, g, b):
            mu = jnp.mean(x, -1, keepdims=True)
            var = jnp.mean(jnp.square(x - mu), -1, keepdims=True)
            return (x - mu) * jax.lax.rsqrt(var + EPS) * g + b
        key = jax.random.key(seed)
        ks = jax.random.split(key, 12)
        s = lambda d: 1.0 / np.sqrt(d)
        return {'x': jax.random.normal(ks[0], (2, 256, DIM), jnp.float32), 'conv_w': jax.random.normal(ks[1], (DIM, DIM, 3), jnp.float32) * s(DIM * 3), 'conv_b': jnp.zeros((DIM,), jnp.float32), 'wqkv': jax.random.normal(ks[2], (3 * DIM, DIM), jnp.float32) * s(DIM), 'bqkv': jnp.zeros((3 * DIM,), jnp.float32), 'wo': jax.random.normal(ks[3], (DIM, DIM), jnp.float32) * s(DIM), 'bo': jnp.zeros((DIM,), jnp.float32), 'ln1_g': jnp.ones((DIM,), jnp.float32), 'ln1_b': jnp.zeros((DIM,), jnp.float32), 'gate_w': jax.random.normal(ks[4], (DIM, EXPERTS), jnp.float32) * s(DIM), 'gate_b': jnp.zeros((EXPERTS,), jnp.float32), 'w1': jax.random.normal(ks[5], (EXPERTS, DIM, DFF), jnp.float32) * s(DIM), 'b1': jnp.zeros((EXPERTS, DFF), jnp.float32), 'w2': jax.random.normal(ks[6], (EXPERTS, DFF, DIM), jnp.float32) * s(DFF), 'b2': jnp.zeros((EXPERTS, DIM), jnp.float32), 'ln2_g': jnp.ones((DIM,), jnp.float32), 'ln2_b': jnp.zeros((DIM,), jnp.float32)}
    _L0_ffn_in = _L0_ffn_setup()
    _d = {'L0_attn_x': _L0_attn_in['x'], 'L0_attn_Wq': _L0_attn_in['Wq'], 'L0_attn_bq': _L0_attn_in['bq'], 'L0_attn_Wk': _L0_attn_in['Wk'], 'L0_attn_bk': _L0_attn_in['bk'], 'L0_attn_Wv': _L0_attn_in['Wv'], 'L0_attn_bv': _L0_attn_in['bv'], 'L0_attn_Wo': _L0_attn_in['Wo'], 'L0_attn_bo': _L0_attn_in['bo'], 'L0_ffn_conv_w': _L0_ffn_in['conv_w'], 'L0_ffn_conv_b': _L0_ffn_in['conv_b'], 'L0_ffn_wqkv': _L0_ffn_in['wqkv'], 'L0_ffn_bqkv': _L0_ffn_in['bqkv'], 'L0_ffn_wo': _L0_ffn_in['wo'], 'L0_ffn_bo': _L0_ffn_in['bo'], 'L0_ffn_ln1_g': _L0_ffn_in['ln1_g'], 'L0_ffn_ln1_b': _L0_ffn_in['ln1_b'], 'L0_ffn_gate_w': _L0_ffn_in['gate_w'], 'L0_ffn_gate_b': _L0_ffn_in['gate_b'], 'L0_ffn_w1': _L0_ffn_in['w1'], 'L0_ffn_b1': _L0_ffn_in['b1'], 'L0_ffn_w2': _L0_ffn_in['w2'], 'L0_ffn_b2': _L0_ffn_in['b2'], 'L0_ffn_ln2_g': _L0_ffn_in['ln2_g'], 'L0_ffn_ln2_b': _L0_ffn_in['ln2_b']}
    _x0 = _d['L0_attn_x']
    _d['L0_attn_x'] = jax.random.normal(jax.random.fold_in(jax.random.key(seed), 1), (8, 512, 128), dtype=_x0.dtype)
    del _x0
    return _d

def reference(L0_attn_x, L0_attn_Wq, L0_attn_bq, L0_attn_Wk, L0_attn_bk, L0_attn_Wv, L0_attn_bv, L0_attn_Wo, L0_attn_bo, L0_ffn_conv_w, L0_ffn_conv_b, L0_ffn_wqkv, L0_ffn_bqkv, L0_ffn_wo, L0_ffn_bo, L0_ffn_ln1_g, L0_ffn_ln1_b, L0_ffn_gate_w, L0_ffn_gate_b, L0_ffn_w1, L0_ffn_b1, L0_ffn_w2, L0_ffn_b2, L0_ffn_ln2_g, L0_ffn_ln2_b):

    def _L0_attn_ref(x, Wq, bq, Wk, bk, Wv, bv, Wo, bo):
        import jax, jax.numpy as jnp
        import numpy as np
        D_MODEL = 128
        NUM_HEADS = 16
        SEG = 64
        DIL = 4
        HEAD_DIM = D_MODEL // NUM_HEADS
        B, S, D = x.shape
        H, hd, seg, r = (NUM_HEADS, HEAD_DIM, SEG, DIL)
        scaling = hd ** (-0.5)
        Q = x @ Wq + bq
        K = x @ Wk + bk
        V = x @ Wv + bv
        pad = -S % seg
        if pad:
            Q = jnp.pad(Q, ((0, 0), (0, pad), (0, 0)))
            K = jnp.pad(K, ((0, 0), (0, pad), (0, 0)))
            V = jnp.pad(V, ((0, 0), (0, pad), (0, 0)))
        n = (S + pad) // seg
        sd = seg // r

        def split(t):
            return t.reshape(B, n, sd, r, H, hd)
        offs = jnp.arange(H) % r
        hidx = jnp.arange(H)
        Qs = split(Q)[:, :, :, offs, hidx, :]
        Ks = split(K)[:, :, :, offs, hidx, :]
        Vs = split(V)[:, :, :, offs, hidx, :]
        scores = jnp.einsum('bnshd,bnshd->bnsh', Qs, Ks) * scaling
        probs = jax.nn.softmax(scores, axis=2)
        attn = probs[..., None] * Vs
        out = jnp.zeros((B, n, sd, r, H, hd), x.dtype)
        out = out.at[:, :, :, offs, hidx, :].set(attn)
        out = out.reshape(B, n * seg, D)[:, :S]
        return out @ Wo + bo

    def _L0_ffn_ref(x, conv_w, conv_b, wqkv, bqkv, wo, bo, ln1_g, ln1_b, gate_w, gate_b, w1, b1, w2, b2, ln2_g, ln2_b):
        import jax, jax.numpy as jnp
        import numpy as np
        DIM, HEADS, EXPERTS, DFF = (128, 16, 8, 512)
        EPS = 1e-05

        def layernorm(x, g, b):
            mu = jnp.mean(x, -1, keepdims=True)
            var = jnp.mean(jnp.square(x - mu), -1, keepdims=True)
            return (x - mu) * jax.lax.rsqrt(var + EPS) * g + b
        B, S, D = x.shape
        H, dh = (HEADS, D // HEADS)
        xt = jnp.transpose(x, (0, 2, 1))
        xt = jax.lax.conv_general_dilated(xt, conv_w, (1,), [(1, 1)], dimension_numbers=('NCH', 'OIH', 'NCH'))
        x = jnp.transpose(xt + conv_b[None, :, None], (0, 2, 1))
        qkv = x @ wqkv.T + bqkv
        q, k, v = jnp.split(qkv, 3, axis=-1)
        q = q.reshape(B, S, H, dh).transpose(0, 2, 1, 3)
        k = k.reshape(B, S, H, dh).transpose(0, 2, 1, 3)
        v = v.reshape(B, S, H, dh).transpose(0, 2, 1, 3)
        scores = jnp.einsum('bhqd,bhkd->bhqk', q, k) / jnp.sqrt(jnp.float32(dh))
        attn = jax.nn.softmax(scores, axis=-1)
        ctx = jnp.einsum('bhqk,bhkd->bhqd', attn, v)
        ctx = ctx.transpose(0, 2, 1, 3).reshape(B, S, D)
        attn_out = ctx @ wo.T + bo
        x = layernorm(x + attn_out, ln1_g, ln1_b)
        probs = jax.nn.softmax(x @ gate_w + gate_b, axis=-1)
        h = jax.nn.relu(jnp.einsum('bsd,edf->bsef', x, w1) + b1)
        y = jnp.einsum('bsef,efd->bsed', h, w2) + b2
        moe_out = jnp.einsum('bse,bsed->bsd', probs, y)
        x = layernorm(x + moe_out, ln2_g, ln2_b)
        return x
    x = L0_attn_x
    x = x + 0.5 * _L0_ffn_ref(_layernorm(x, axis=-1), L0_ffn_conv_w, L0_ffn_conv_b, L0_ffn_wqkv, L0_ffn_bqkv, L0_ffn_wo, L0_ffn_bo, L0_ffn_ln1_g, L0_ffn_ln1_b, L0_ffn_gate_w, L0_ffn_gate_b, L0_ffn_w1, L0_ffn_b1, L0_ffn_w2, L0_ffn_b2, L0_ffn_ln2_g, L0_ffn_ln2_b)
    x = x + _L0_attn_ref(_layernorm(x, axis=-1), L0_attn_Wq, L0_attn_bq, L0_attn_Wk, L0_attn_bk, L0_attn_Wv, L0_attn_bv, L0_attn_Wo, L0_attn_bo)
    x = x + 0.5 * _L0_ffn_ref(_layernorm(x, axis=-1), L0_ffn_conv_w, L0_ffn_conv_b, L0_ffn_wqkv, L0_ffn_bqkv, L0_ffn_wo, L0_ffn_bo, L0_ffn_ln1_g, L0_ffn_ln1_b, L0_ffn_gate_w, L0_ffn_gate_b, L0_ffn_w1, L0_ffn_b1, L0_ffn_w2, L0_ffn_b2, L0_ffn_ln2_g, L0_ffn_ln2_b)
    return x

_drawn_inputs = setup_inputs


def setup_inputs(seed=0):
    import zlib

    import numpy as np

    out = dict(_drawn_inputs(seed))
    spreads = {'L0_attn_bq': (0.0, 2.0),
     'L0_attn_bk': (0.0, 0.8),
     'L0_attn_bv': (0.0, 0.8),
     'L0_attn_bo': (0.0, 0.1),
     'L0_ffn_conv_b': (0.0, 0.1),
     'L0_ffn_bqkv': (0.0, 0.1),
     'L0_ffn_bo': (0.0, 0.1),
     'L0_ffn_ln1_g': (1.0, 0.2),
     'L0_ffn_ln1_b': (0.0, 0.1),
     'L0_ffn_gate_b': (0.0, 0.417),
     'L0_ffn_b1': (0.0, 0.354),
     'L0_ffn_b2': (0.0, 0.269),
     'L0_ffn_ln2_g': (1.0, 0.2),
     'L0_ffn_ln2_b': (0.0, 0.1)}
    factors = {}
    for name, (base, spread) in spreads.items():
        noise = np.random.default_rng([zlib.crc32(name.encode()), seed]).standard_normal(out[name].shape)
        drawn = base * np.exp(spread * noise) if base else spread * noise
        out[name] = jnp.asarray(drawn.astype(out[name].dtype))
    for name, factor in factors.items():
        out[name] = (out[name] * factor).astype(out[name].dtype)
    return out
```

```python
from contextlib import ExitStack

import numpy as np

import concourse.bass as bass
from concourse import mybir

ALU = mybir.AluOpType
ACT = mybir.ActivationFunctionType
AX = mybir.AxisListType
F32 = mybir.dt.float32
F32R = mybir.dt.float32r
BF16 = mybir.dt.bfloat16

B, S, D = 8, 512, 128
H, DH = 16, 8
E, FF = 8, 512
TC = S // 128
FC = FF // 128
G, HG = 4, 4
SEG, DIL = 64, 4
EPS = 1e-5
SCALE = float(DH) ** -0.5
UNITS = 2 * B

PART_OF_ROW = ((0, 0, 0, 1, 1, 2), (0, 1, 2, 0, 1, 0))
PAIRS = len(PART_OF_ROW[0])
SCORE_ROWS = 96
MAX_ROW = 96
ALL_ROWS = 128

TICKS = 64
P2_AT = 24
PV_LAG = 5
EXPERTS_AT = 108
MID_FIRST = 6


class Unit:

    def __init__(self, number, parity):
        self.n, self.parity = number, parity

    def count(self, per_unit, k):
        return per_unit * self.n + k


def wait(eng, sem, value):
    if isinstance(value, int) and value <= 0:
        return
    eng.wait_ge(sem, value)


def macaron(nc, x, Wq, bq, Wk, bk, Wv, bv, Wo, bo, conv_w, conv_b, wqkv, bqkv, wo, bo2, ln1_g, ln1_b,
            gate_w, gate_b, w1, b1, w2, b2, ln2_g, ln2_b, out):
    with ExitStack() as ctx:
        def sb(name, shape, dt=F32):
            return ctx.enter_context(nc.sbuf_tensor(name, shape, dt))

        def psum(name):
            return ctx.enter_context(nc.psum_tensor(name, [128, 512], F32))

        def sem(name):
            return ctx.enter_context(nc.semaphore(name))

        score1 = [psum("score1a"), psum("score1b")]
        score2 = [psum("score2a"), psum("score2b")]
        ctx_ps = psum("ctx_ps")
        hid_ps = psum("hid_ps")
        y_ps = psum("y_ps")
        misc = psum("misc")

        xs = sb("xs", [128, B * S])
        w1h, w1l = sb("w1h", [128, E * FF], F32R), sb("w1l", [128, E * FF], F32R)
        w2s = sb("w2s", [128, E * FC, D])
        b2s = sb("b2s", [E, D])
        gws = sb("gws", [128, E])
        cwh, cwl = sb("cwh", [128, 3, D], F32R), sb("cwl", [128, 3, D], F32R)
        qkh, qkl = sb("qkh", [128, 2, D], F32R), sb("qkl", [128, 2, D], F32R)
        wvT, woT = sb("wvT", [128, D]), sb("woT", [128, D])
        mwh, mwl = sb("mwh", [128, 3, D], F32R), sb("mwl", [128, 3, D], F32R)
        mwo = sb("mwo", [128, D])
        NV = E * FC + 9
        cols = sb("cols", [128, NV])
        (V_CONV, V_BQ, V_BK, V_G1, V_B1, V_MBQ, V_MBK, V_MBV) = range(E * FC, E * FC + 8)
        names = ["bv_b", "bo_b", "g1_b", "b1_b", "g2_b", "b2_b", "mbo_b"]
        bv_b, bo_b, g1_b, b1_b, g2_b, b2_b, mbo_b = (sb(n, [128, D]) for n in names)
        gb_b = sb("gb_b", [128, E])
        ident, heads8 = sb("ident", [128, 128]), sb("heads8", [128, 128])
        dil_mask = sb("dil_mask", [128, DIL])
        minus_half, eps_t = sb("minus_half", [128, TC]), sb("eps_t", [128, TC])
        f_xn = sb("f_xn", [128, S])
        xh, xl = sb("xh", [128, S + 2], F32R), sb("xl", [128, S + 2], F32R)
        ch = [sb(f"ch{p}", [128, S], F32R) for p in range(2)]
        cl = [sb(f"cl{p}", [128, S], F32R) for p in range(2)]
        parts = [sb("q_parts", [128, 3, S], BF16), sb("k_parts", [128, 3, S], BF16)]
        rest = sb("rest", [128, S])
        Qp, Kp = sb("Qp", [128, H, S], BF16), sb("Kp", [128, H, S], BF16)
        V = [sb(f"V{p}", [128, TC, H, DH + 1]) for p in range(2)]
        negmax = sb("negmax", [128, 2, HG * TC])
        m_parts, m_rest = sb("m_parts", [HG * TC, 3, 128], BF16), sb("m_rest", [HG * TC, 128])
        probs = sb("probs", [128, 2, HG, S])
        ctxT = sb("ctxT", [128, S])
        rden = sb("rden", [128, TC, HG])
        ctxs = sb("ctxs", [128, TC, H, DH])
        x1n = sb("x1n", [128, S])
        x1h = [sb(f"x1h{p}", [128, S], F32R) for p in range(2)]
        x1l = [sb(f"x1l{p}", [128, S], F32R) for p in range(2)]
        x1f, x1t = sb("x1f", [128, S]), sb("x1t", [128, S])
        lg, lg2, eg = sb("lg", [128, TC, E]), sb("lg2", [128, TC, E]), sb("eg", [128, TC, E])
        gmax, gsum, ginv = sb("gmax", [128, TC]), sb("gsum", [128, TC]), sb("ginv", [128, TC])
        gate = [sb(f"gate{p}", [128, TC, E]) for p in range(2)]
        gateT = sb("gateT", [E, S])
        hid = sb("hid", [128, 2, FC, S])
        yacc = [sb(f"yacc{p}", [128, S]) for p in range(2)]
        zn = sb("zn", [128, S])
        m_xn = sb("m_xn", [128, S])
        mxh, mxl = sb("mxh", [128, S], F32R), sb("mxl", [128, S], F32R)
        mq = sb("mq", [128, S])
        NSG = S // SEG
        mmax, msum, minv, mwt = (sb(n, [128, NSG, DIL]) for n in ("mmax", "msum", "minv", "mwt"))
        ln = {k: (sb(f"{k}_st", [128, TC, 6]), sb(f"{k}_mv", [128, TC, 2]), sb(f"{k}_ve", [128, TC]),
                  sb(f"{k}_rs", [128, TC])) for k in ("f", "c", "e", "m")}
        stage = probs[:].rearrange("p a j q -> p (a j q)")
        conv_raw = stage[:, 0:3 * D].rearrange("p (i j) -> p i j", j=3)
        wqkv_raw = stage[:, 3 * D:6 * D].rearrange("p (j i) -> p j i", j=3)
        mws = stage[:, 6 * D:9 * D].rearrange("p (j i) -> p j i", j=3)
        wo_raw = stage[:, 9 * D:10 * D]
        vec_rows = stage[0:NV, 10 * D:11 * D]
        dram = [nc.dram_tensor(f"{n}_dram", [3, H, DH, S], BF16).ap() for n in ("q_parts", "k_parts")]

        s = {}
        for n in """
            ld_x0 ld_x ld_vec ld_small ld_conv ld_qkv ld_wo ld_mid ld_w1 ld_w2 ld_bc
            zero_v pack_zero ident0 ident_ready held_dve held_sp heads0 heads1 heads_ready mask_ready g2_half
            set_vT set_cols set_cT set_ch set_cl set_qT set_qh set_ql set_wv set_oT set_wo set_mh set_ml
            set_w1h set_w1l
            f_bn f_mv f_ve f_rs c_bn c_mv c_ve c_rs e_bn e_mv e_ve e_rs m_bn m_mv m_ve m_rs
            f_xn f_xT f_xh f_xl f_conv f_ch f_cl f_qk f_p1 f_r1 f_p2 f_p3 f_v f_vs parts_out pack_in
            a_s1 a_max a_nmT a_m1 a_r1 a_m2 a_m3 a_m_in a_s2 a_exp a_pv a_ctx a_ctxT a_rden a_norm
            c_cT c_cTs c_x1 c_x1p c_xn c_xnT c_x1h c_x1f c_x1l c_x1g c_x1t
            c_gate c_lg c_gmax c_lg2 c_eg c_gsum c_ginv c_pr c_prT c_prTs c_b2 c_y0
            h_mm h_relu y_mm y_acc
            e_zn e_zg e_zb e_x
            m_xn m_xT m_xh m_xl m_q m_mq m_k m_qk m_s m_max m_sc m_ex m_sum m_inv m_wt m_w m_v m_o m_out m_t
            m_x x_out
        """.split():
            assert n not in s, n
            s[n] = sem(n)

        def col(k):
            return cols[:, k:k + 1]

        def chunk(ap, c):
            return ap[:, c * 128:(c + 1) * 128]

        def slot(u, c=0, n=TC):
            at = u % B * S + c * 128
            return xs[:, at:at + n * 128] if isinstance(at, int) else xs[:, bass.ds(at, n * 128)]

        LAST_UNIT = UNITS - 1
        misc_uses = sorted(
            [(17 + 16 * g - TICKS * b, b, "a_m3r", 4, g + 1) for g, b in ((0, 0), (1, 0), (2, 0), (3, 1))]
            + [(44 + 16 * g - TICKS * b, b, "a_norm", 4, g + 1) for g, b in ((0, 0), (1, 0), (2, 1), (3, 1))]
            + [(31, 1, "c_cTs", 1, 1), (34, 1, "c_x1p", 1, 1), (40, 1, "c_x1f", 1, 1), (46, 1, "c_lg", 1, 1),
               (51, 1, "c_prTs", 1, 1), (53, 1, "c_y0", 1, 1)]
            + [(26, -1, "f_xl", 1, 1), (36, -1, "f_cl", 1, 1), (38, -1, "f_r1", 2, 1), (42, -1, "f_r1", 2, 2),
               (55, -1, "f_vs", 1, 1)]
            + [(5, "mid", "m_xl", 1, 1), (7, "mid", "m_mq", 1, 1), (9, "mid", "m_qk", 1, 1),
               (14, "mid", "m_sc", 1, 1), (21, "mid", "m_o", 1, 1), (23, "mid", "m_t", 1, 1)],
            key=lambda use: use[0])

        def in_iteration(i0, back):
            if back == "mid":
                return MID_FIRST <= i0 < MID_FIRST + B
            return 0 <= i0 - back <= LAST_UNIT

        def wait_misc(pe, tick, i, i0):
            before = [(t, b, n, per, k, 0) for t, b, n, per, k in misc_uses if t < tick]
            earlier = [(t, b, n, per, k, 1) for t, b, n, per, k in misc_uses]
            for t, b, n, per, k, ago in reversed(earlier + before):
                if in_iteration(i0 - ago, b):
                    u = i - ago - (MID_FIRST if b == "mid" else b)
                    name = "a_r1" if n == "a_m3r" else n
                    wait(pe, s[name], per * u + k)
                    return
            wait(pe, s["set_mh"], 1)
            wait(pe, s["set_wo"], 1)

        def run(eng, iteration):
            for i in (-1, 0, 1):
                iteration(i, i % 2, i)
            for a, b in ((2, MID_FIRST), (MID_FIRST, MID_FIRST + B)):
                with eng.Fori(a, b, 2) as r:
                    iteration(r, 0, a + 2)
                    iteration(r + 1, 1, a + 3)
            for i in (14, 15, 16, 17):
                iteration(i, i % 2, i)

        def walk(i, parity, i0, unit_tick, mid_tick=None):
            for t in range(TICKS):
                if mid_tick and in_iteration(i0, "mid"):
                    mid_tick(t, Unit(i - MID_FIRST, parity), i, i0)
                for back in (2, 1, 0, -1):
                    if in_iteration(i0, back):
                        unit_tick(t + TICKS * back, Unit(i - back, (parity - back) % 2), t, i, i0)

        NM_AT = {17 + 16 * g: g for g in range(G)}
        CTX_AT = {44 + 16 * g: g for g in range(G)}
        LOADS_AT = {-16: 0, -6: 1, 9: 2, 25: 3}

        block = ctx.enter_context(nc.Block())

        @block.sync
        def _(sp):
            def load(dst, src, name):
                sp.dma_start(dst, src).then_inc(s[name], 16)

            def row(v):
                return v.rearrange("(a n) -> a n", a=1)

            load(xs[:, 0:S].rearrange("p (c d) -> p c d", c=TC), x[0].rearrange("(c p) d -> p c d", p=128), "ld_x0")
            for r in range(0, E):
                load(vec_rows[r * FC:(r + 1) * FC, :], b1[r].rearrange("(f p) -> f p", p=128), "ld_vec")
            load(vec_rows[V_CONV:V_CONV + 1, :], row(conv_b), "ld_vec")
            load(vec_rows[V_BQ:V_BQ + 2, :], bqkv[0:2 * D].rearrange("(a n) -> a n", a=2), "ld_vec")
            for k, v in ((V_G1, ln1_g), (V_B1, ln1_b), (V_MBQ, bq), (V_MBK, bk), (V_MBV, bv), (NV - 1, bv)):
                load(vec_rows[k:k + 1, :], row(v), "ld_vec")
            load(conv_raw, conv_w, "ld_conv")
            load(wqkv_raw, wqkv.rearrange("(j o) i -> o j i", j=3), "ld_qkv")
            load(wo_raw, wo, "ld_wo")
            for k, v in enumerate((Wq, Wk, Wv)):
                load(mws[:, k, :], v, "ld_mid")
            for dst, v in ((bv_b, bqkv[2 * D:3 * D]), (bo_b, bo2), (g1_b, ln1_g), (b1_b, ln1_b), (g2_b, ln2_g),
                           (b2_b, ln2_b), (mbo_b, bo)):
                load(dst[:], v.partition_broadcast(128), "ld_bc")
            load(gb_b[:], gate_b.partition_broadcast(128), "ld_bc")
            load(mwo[:], Wo, "ld_small")
            load(gws[:], gate_w, "ld_small")
            load(b2s[:], b2, "ld_small")
            for b in range(1, B):
                load(xs[:, b * S:(b + 1) * S].rearrange("p (c d) -> p c d", c=TC),
                     x[b].rearrange("(c p) d -> p c d", p=128), "ld_x")
            for e in range(E):
                load(hid[:, e // FC, e % FC, :], w1[e], "ld_w1")
            for e in range(E):
                load(w2s[:, e * FC:(e + 1) * FC, :], w2[e].rearrange("(f p) d -> p f d", p=128), "ld_w2")

            def wait_sp(sem, value):
                wait(sp, sem, value)
                sp.sem_inc(s["held_sp"], 1)

            def tick(T, u, t, i, i0):
                for k, at in ((0, 40 - TICKS), (1, 44 - TICKS)):
                    if T == at:
                        wait_sp(s["f_p3"], u.count(2, k + 1))
                        wait_sp(s["pack_in"], u.count(192 * G, 0))
                        sp.dma_start(dram[k].rearrange("a h d q -> (h d) a q"), parts[k][:]).then_inc(s["parts_out"], 16)
                if T in LOADS_AT:
                    g = LOADS_AT[T]
                    wait_sp(s["parts_out"], u.count(32, 32))
                    wait_sp(s["a_s2"], (u.n - 1) * 64 + 16 * g + 16)
                    wait_sp(s["pack_zero"], 1)
                    wait_sp(s["pack_in"], u.count(192 * G, 192 * g))
                    hs = slice(g * HG, (g + 1) * HG)
                    for k, packed in ((0, Qp), (1, Kp)):
                        for row, part in enumerate(PART_OF_ROW[k]):
                            sp.dma_start(packed[row * DH:(row + 1) * DH, hs, :],
                                         dram[k][part, hs, :, :].rearrange("h d q -> d h q"))\
                                .then_inc(s["pack_in"], 16)
                if T - 2 in NM_AT:
                    g = NM_AT[T - 2]
                    wait_sp(s["a_m3"], u.count(4, g + 1))
                    wait_sp(s["pack_zero"], 1)
                    for part in range(3):
                        sp.dma_start(Qp[MAX_ROW + part:MAX_ROW + part + 1, g * HG:(g + 1) * HG, :],
                                     m_parts[:, part, :]).then_inc(s["a_m_in"], 16)
                if T == 190 and i0 >= 15:
                    first = {15: B, 16: 14, 17: 15}[i0]
                    wait_sp(s["e_x"], i0 - 1)
                    for b in range(first, i0 - 1):
                        sp.dma_start(out[b - B].rearrange("(c p) d -> p c d", p=128),
                                     xs[:, (b - B) * S:(b - B + 1) * S].rearrange("p (c d) -> p c d", c=TC))\
                            .then_inc(s["x_out"], 16)

            run(sp, lambda i, p, i0: walk(i, p, i0, tick))
            sp.wait_ge(s["x_out"], 16 * B)

        @block.gpsimd
        def _(pool):
            pool.memset(ident[:], 0.0).then_inc(s["ident0"], 1)
            pool.wait_ge(s["ident0"], 1)
            pool.affine_select(out=ident[:], in_=ident[:], compare_op=ALU.not_equal, fill=1.0, base=0,
                               pattern=[[-1, 128]], channel_multiplier=1).then_inc(s["ident_ready"], 1)
            pool.memset(minus_half[:], -0.5).then_inc(s["heads0"], 1)
            pool.memset(eps_t[:], EPS).then_inc(s["heads0"], 1)
            pool.memset(heads8[:], 1.0).then_inc(s["heads0"], 1)
            pool.wait_ge(s["heads0"], 3)
            blocks = heads8[:].rearrange("p (h d) -> p h d", d=DH)
            pool.affine_select(out=blocks, in_=blocks, compare_op=ALU.is_ge, fill=0.0, base=0,
                               pattern=[[-DH, H], [0, DH]], channel_multiplier=1).then_inc(s["heads1"], 1)
            pool.wait_ge(s["heads1"], 1)
            pool.affine_select(out=blocks, in_=blocks, compare_op=ALU.is_ge, fill=0.0, base=DH - 1,
                               pattern=[[DH, H], [0, DH]], channel_multiplier=-1).then_inc(s["heads_ready"], 1)
            pool.wait_ge(s["ld_bc"], 16 * 8)
            pool.tensor_scalar(g2_b[:], g2_b[:], 0.5, None, ALU.mult).then_inc(s["g2_half"], 1)
            pool.tensor_scalar(b2_b[:], b2_b[:], 0.5, None, ALU.mult).then_inc(s["g2_half"], 1)

            def inv_std(key, n):
                _, mv, ve, rs = ln[key]
                wait(pool, s[f"{key}_mv"], n + 1)
                pool.tensor_tensor(ve[:], mv[:, :, 1], eps_t[:], ALU.add).then_inc(s[f"{key}_ve"], 1)
                wait(pool, s[f"{key}_ve"], n + 1)
                pool.tensor_tensor(ve[:], ve[:], minus_half[:], ALU.pow).then_inc(s[f"{key}_rs"], 1)

            def per_chunk(v):
                return v[:].unsqueeze(1).to_broadcast([128, TC, D])

            def tick(T, u, t, i, i0):
                if T == 22 - TICKS:
                    inv_std("f", u.n)
                if T == 100:
                    inv_std("c", u.n)
                if T == 104:
                    wait(pool, s["c_xn"], u.count(1, 1))
                    wait(pool, s["c_y0"], u.count(1, 0))
                    pool.tensor_tensor(x1t[:].rearrange("p (c d) -> p c d", c=TC),
                                       x1n[:].rearrange("p (c d) -> p c d", c=TC), per_chunk(g1_b), ALU.mult)\
                        .then_inc(s["c_x1g"], 1)
                    wait(pool, s["c_x1g"], u.count(1, 1))
                    pool.tensor_tensor(x1t[:].rearrange("p (c d) -> p c d", c=TC),
                                       x1t[:].rearrange("p (c d) -> p c d", c=TC), per_chunk(b1_b), ALU.add)\
                        .then_inc(s["c_x1t"], 1)
                if T == 181:
                    inv_std("e", u.n)
                if T == 183:
                    wait(pool, s["e_zn"], u.count(1, 1))
                    wait(pool, s["g2_half"], 2)
                    pool.tensor_tensor(zn[:].rearrange("p (c d) -> p c d", c=TC),
                                       zn[:].rearrange("p (c d) -> p c d", c=TC), per_chunk(g2_b), ALU.mult)\
                        .then_inc(s["e_zg"], 1)
                    wait(pool, s["e_zg"], u.count(1, 1))
                    pool.tensor_tensor(zn[:].rearrange("p (c d) -> p c d", c=TC),
                                       zn[:].rearrange("p (c d) -> p c d", c=TC), per_chunk(b2_b), ALU.add)\
                        .then_inc(s["e_zb"], 1)

            def mid(t, b, i, i0):
                if t == 1:
                    inv_std("m", b.n)

            run(pool, lambda i, p, i0: walk(i, p, i0, tick, mid))

        @block.scalar
        def _(act):
            act.wait_ge(s["set_cT"], 1)
            act.activation(cwh[:].rearrange("p j o -> p (j o)"), misc[:, 0:3 * D], ACT.Copy).then_inc(s["set_ch"], 1)
            act.wait_ge(s["set_qT"], 1)
            act.activation(qkh[:].rearrange("p j o -> p (j o)"), misc[:, 0:2 * D], ACT.Copy).then_inc(s["set_qh"], 1)
            act.wait_ge(s["ld_mid"], 48)
            act.activation(mwh[:], mws, ACT.Copy).then_inc(s["set_mh"], 1)
            act.wait_ge(s["set_cols"], 1)

            def split_w1():
                act.wait_ge(s["ld_w1"], 16 * E)
                for e in range(E):
                    act.activation(w1h[:, e * FF:(e + 1) * FF], hid[:, e // FC, e % FC, :], ACT.Copy)\
                        .then_inc(s["set_w1h"], 1)

            def tick(T, u, t, i, i0):
                if T == 26 - TICKS:
                    wait(act, s["f_xT"], u.count(1, 1))
                    wait(act, s["f_conv"], u.count(1, 0))
                    wait(act, s["zero_v"], 1)
                    act.activation(xh[:, 1:S + 1], misc[:], ACT.Copy).then_inc(s["f_xh"], 1)
                if T == 36 - TICKS:
                    wait(act, s["f_conv"], u.count(1, 1))
                    wait(act, s["c_x1"], u.n - 1)
                    act.activation(ch[u.parity][:], misc[:], ACT.Identity, bias=col(V_CONV)).then_inc(s["f_ch"], 1)
                for k, at, bias in ((0, 38 - TICKS, V_BQ), (1, 42 - TICKS, V_BK)):
                    if T == at:
                        wait(act, s["f_qk"], u.count(2, k + 1))
                        wait(act, s["parts_out"], u.count(32, 0))
                        act.activation(parts[k][:, 0, :], misc[:], ACT.Identity, bias=col(bias))\
                            .then_inc(s["f_p1"], 1)
                    if T == at + 1:
                        wait(act, s["f_r1"], u.count(2, k + 1))
                        act.activation(parts[k][:, 1, :], rest[:], ACT.Copy).then_inc(s["f_p2"], 1)
                if T in NM_AT:
                    g = NM_AT[T]
                    wait(act, s["a_nmT"], u.count(4, g + 1))
                    wait(act, s["a_m_in"], u.count(48 * G, 48 * g))
                    act.activation(m_parts[:, 0, :], misc[0:HG * TC, 0:128], ACT.Copy).then_inc(s["a_m1"], 1)
                if T - 1 in NM_AT:
                    g = NM_AT[T - 1]
                    wait(act, s["a_r1"], u.count(4, g + 1))
                    act.activation(m_parts[:, 1, :], m_rest[:], ACT.Copy).then_inc(s["a_m2"], 1)
                if P2_AT <= T < P2_AT + 64:
                    n, j = divmod(T - P2_AT, HG)
                    wait(act, s["a_s2"], u.count(64, T - P2_AT + 1))
                    wait(act, s["a_pv"], u.count(16, n - 1))
                    act.activation(probs[:, n % 2, j, :], score2[(T - P2_AT) % 2][:], ACT.Exp, scale=SCALE)\
                        .then_inc(s["a_exp"], 1)
                if T - 42 in (0, 16, 32, 48):
                    g = (T - 42) // 16
                    wait(act, s["a_pv"], u.count(16, 4 * g + 4))
                    wait(act, s["a_ctxT"], u.count(4, g))
                    wait(act, s["c_x1"], u.n)
                    act.activation(ctxT[:], ctx_ps[:], ACT.Copy).then_inc(s["a_ctx"], 1)
                if T == 95:
                    wait(act, s["c_cT"], u.count(1, 1))
                    act.activation(ctxT[:], misc[:], ACT.Copy).then_inc(s["c_cTs"], 1)
                if T == 104:
                    wait(act, s["c_xnT"], u.count(1, 1))
                    wait(act, s["h_mm"], (u.n - 1) * 32 + 1)
                    act.activation(x1h[u.parity][:], misc[:], ACT.Identity, bias=col(V_B1), scale=col(V_G1))\
                        .then_inc(s["c_x1h"], 1)
                if T == 111:
                    wait(act, s["c_lg2"], u.count(1, 1))
                    act.activation(eg[:], lg2[:], ACT.Exp).then_inc(s["c_eg"], 1)
                if T == 115:
                    wait(act, s["c_prT"], u.count(1, 1))
                    act.activation(gateT[:], misc[0:E, :], ACT.Copy).then_inc(s["c_prTs"], 1)
                m = T - EXPERTS_AT
                if 0 <= m < 64 and m % 2 == 0:
                    n = m // 2
                    e, f = divmod(n, FC)
                    wait(act, s["h_mm"], u.count(32, n + 1))
                    wait(act, s["set_w1l"], E)
                    wait(act, s["y_mm"], u.count(8, e - 1))
                    act.activation(hid[:, e % 2, f, :], hid_ps[:], ACT.Relu, bias=col(n)).then_inc(s["h_relu"], 1)

            def mid(t, b, i, i0):
                if t == 5:
                    wait(act, s["m_xT"], b.count(1, 1))
                    act.activation(mxh[:], misc[:], ACT.Copy).then_inc(s["m_xh"], 1)
                if t == 7:
                    wait(act, s["m_q"], b.count(1, 1))
                    act.activation(mq[:], misc[:], ACT.Identity, bias=col(V_MBQ)).then_inc(s["m_mq"], 1)
                if t == 15:
                    wait(act, s["m_sc"], b.count(1, 1))
                    act.activation(m_xn[:], m_xn[:], ACT.Exp, scale=SCALE).then_inc(s["m_ex"], 1)

            def iteration(i, p, i0):
                if i0 == 0:
                    split_w1()
                    act.wait_ge(s["set_oT"], 1)
                    act.wait_ge(s["set_ml"], 1)
                walk(i, p, i0, tick, mid)

            run(act, iteration)

        @block.vector
        def _(dve):
            dve.memset(Kp[:].bitcast(F32), 0.0)
            dve.memset(Qp[:].bitcast(F32), 0.0)
            for p in range(2):
                dve.memset(V[p][:], 1.0)
            for z in (xh, xl):
                dve.memset(z[:].bitcast(F32), 0.0)
            dve.memset(ctx_ps[:], 0.0).then_inc(s["zero_v"], 1)
            dve.wait_ge(s["zero_v"], 1)
            dve.memset(Kp[MAX_ROW:MAX_ROW + 3, :, :], 1.0).then_inc(s["pack_zero"], 1)
            dve.wait_ge(s["set_vT"], 1)
            dve.tensor_copy(cols[:], misc[:, 0:NV]).then_inc(s["set_cols"], 1)
            dve.wait_ge(s["set_ch"], 1)
            dve.tensor_tensor(cwl[:].rearrange("p j o -> p (j o)"), misc[:, 0:3 * D],
                              cwh[:].bitcast(F32).rearrange("p j o -> p (j o)"), ALU.subtract)\
                .then_inc(s["set_cl"], 1)
            dve.wait_ge(s["set_qh"], 1)
            dve.tensor_tensor(qkl[:].rearrange("p j o -> p (j o)"), misc[:, 0:2 * D],
                              qkh[:].bitcast(F32).rearrange("p j o -> p (j o)"), ALU.subtract)
            dve.tensor_copy(wvT[:], misc[:, 2 * D:3 * D]).then_inc(s["set_ql"], 1)
            dve.wait_ge(s["set_oT"], 1)
            dve.tensor_copy(woT[:], misc[:, 0:D]).then_inc(s["set_wo"], 1)
            dve.wait_ge(s["set_mh"], 1)
            dve.tensor_tensor(mwl[:], mws, mwh[:].bitcast(F32), ALU.subtract).then_inc(s["set_ml"], 1)
            dve.wait_ge(s["heads_ready"], 1)
            dve.tensor_reduce(dil_mask[:], heads8[:].rearrange("p (a r d) -> p r a d", r=DIL, d=DH), AX.XY,
                              ALU.max).then_inc(s["mask_ready"], 1)
            dve.wait_ge(s["ld_bc"], 16 * 8)
            dve.sem_inc(s["m_x"], 1)

            def split_w1():
                for e in range(E):
                    dve.wait_ge(s["set_w1h"], e + 1)
                    dve.tensor_tensor(w1l[:, e * FF:(e + 1) * FF], hid[:, e // FC, e % FC, :],
                                      w1h[:, e * FF:(e + 1) * FF].bitcast(F32), ALU.subtract)\
                        .then_inc(s["set_w1l"], 1)

            def moments(key, n, src):
                st, mv, _, _ = ln[key]
                for c in range(TC):
                    last = dve.bn_stats(st[:, c, :], src(c))
                last.then_inc(s[f"{key}_bn"], 1)
                wait(dve, s[f"{key}_bn"], n + 1)
                dve.sem_inc(s["held_dve"], 1)
                for c in range(TC):
                    last = dve.bn_aggr(mv[:, c, :], st[:, c, :])
                last.then_inc(s[f"{key}_mv"], 1)

            def normalise(key, n, dst, src, done):
                _, mv, rs, _ = ln[key]
                wait(dve, s[f"{key}_rs"], n + 1)
                for c in range(TC):
                    last = dve.tensor_scalar(chunk(dst, c), src(c), mv[:, c, 0:1], rs[:, c:c + 1],
                                             ALU.subtract, ALU.mult)
                last.then_inc(s[done], 1)

            def tick(T, u, t, i, i0):
                m = T - EXPERTS_AT - 15
                if 0 <= m < 64 and m % 8 == 0:
                    e = m // 8
                    wait(dve, s["y_mm"], u.count(8, e + 1))
                    wait(dve, s["c_y0"], u.count(1, 1))
                    wait(dve, s["y_acc"], u.count(8, e))
                    ya = yacc[u.parity]
                    for c in range(TC):
                        last = dve.scalar_tensor_tensor(out=chunk(ya, c), in0=chunk(y_ps, c),
                                                        scalar=gate[u.parity][:, c, e:e + 1], in1=chunk(ya, c),
                                                        op0=ALU.mult, op1=ALU.add)
                    last.then_inc(s["y_acc"], 1)
                if T == 180:
                    wait(dve, s["y_acc"], u.count(8, 8))
                    moments("e", u.n, lambda c: chunk(yacc[u.parity], c))
                if T == 182:
                    normalise("e", u.n, zn, lambda c: chunk(yacc[u.parity], c), "e_zn")
                if T == 186:
                    wait(dve, s["e_zb"], u.count(1, 1))
                    dve.tensor_tensor(slot(u.n), slot(u.n), zn[:], ALU.add).then_inc(s["e_x"], 1)
                if 0 <= T < 64:
                    h, qc = divmod(T, TC)
                    g = h // HG
                    wait(dve, s["a_s1"], u.count(64, T + 1))
                    if T % 16 == 0:
                        wait(dve, s["a_nmT"], u.count(4, g - 1))
                    dve.tensor_reduce(negmax[:, g % 2, T % 16:T % 16 + 1], score1[T % 2][:], AX.X, ALU.max,
                                      negate=True).then_inc(s["a_max"], 1)
                if T in NM_AT:
                    g = NM_AT[T]
                    wait(dve, s["a_m1"], u.count(4, g + 1))
                    dve.tensor_tensor(m_rest[:], misc[0:HG * TC, 0:128], m_parts[:, 0, :], ALU.subtract)\
                        .then_inc(s["a_r1"], 1)
                if T - 1 in NM_AT:
                    g = NM_AT[T - 1]
                    wait(dve, s["a_m2"], u.count(4, g + 1))
                    dve.tensor_tensor(m_parts[:, 2, :], m_rest[:], m_parts[:, 1, :], ALU.subtract)\
                        .then_inc(s["a_m3"], 1)
                if T in CTX_AT:
                    g = CTX_AT[T]
                    turned = misc[:].rearrange("p (c j r) -> p c j r", c=TC, j=HG)
                    wait(dve, s["a_ctxT"], u.count(4, g + 1))
                    wait(dve, s["c_cT"], u.count(1, 0))
                    dve.reciprocal(rden[:], turned[:, :, :, DH]).then_inc(s["a_rden"], 1)
                    wait(dve, s["a_rden"], u.count(4, g + 1))
                    dve.tensor_tensor(ctxs[:, :, g * HG:(g + 1) * HG, :], turned[:, :, :, 0:DH],
                                      rden[:].unsqueeze(3).to_broadcast([128, TC, HG, DH]), ALU.mult)\
                        .then_inc(s["a_norm"], 1)
                if T == 98:
                    wait(dve, s["c_x1"], u.count(1, 1))
                    wait(dve, s["c_x1g"], u.count(1, 0))
                    dve.tensor_tensor(x1n[:].rearrange("p (c d) -> p c d", c=TC),
                                      misc[:].rearrange("p (c d) -> p c d", c=TC),
                                      bo_b[:].unsqueeze(1).to_broadcast([128, TC, D]), ALU.add)\
                        .then_inc(s["c_x1p"], 1)
                if T == 99:
                    wait(dve, s["c_x1p"], u.count(1, 1))
                    moments("c", u.n, lambda c: chunk(x1n, c))
                if T == 101:
                    normalise("c", u.n, x1n, lambda c: chunk(x1n, c), "c_xn")
                if T == 104:
                    wait(dve, s["c_x1h"], u.count(1, 1))
                    wait(dve, s["c_gate"], u.count(1, 0))
                    dve.tensor_scalar(x1f[:], misc[:], col(V_G1), col(V_B1), ALU.mult, ALU.add)\
                        .then_inc(s["c_x1f"], 1)
                if T == 105:
                    wait(dve, s["c_x1f"], u.count(1, 1))
                    dve.tensor_tensor(x1l[u.parity][:], x1f[:], x1h[u.parity][:].bitcast(F32), ALU.subtract)\
                        .then_inc(s["c_x1l"], 1)
                if T == 110:
                    wait(dve, s["c_gate"], u.count(1, 1))
                    dve.tensor_tensor(lg[:], misc[:, 0:TC * E].rearrange("p (c e) -> p c e", c=TC),
                                      gb_b[:].unsqueeze(1).to_broadcast([128, TC, E]), ALU.add)\
                        .then_inc(s["c_lg"], 1)
                    wait(dve, s["c_lg"], u.count(1, 1))
                    dve.tensor_reduce(gmax[:], lg[:], AX.X, ALU.max).then_inc(s["c_gmax"], 1)
                    wait(dve, s["c_gmax"], u.count(1, 1))
                    dve.tensor_tensor(lg2[:], lg[:], gmax[:].unsqueeze(2).to_broadcast([128, TC, E]),
                                      ALU.subtract).then_inc(s["c_lg2"], 1)
                if T == 112:
                    wait(dve, s["c_eg"], u.count(1, 1))
                    dve.tensor_reduce(gsum[:], eg[:], AX.X, ALU.add).then_inc(s["c_gsum"], 1)
                    wait(dve, s["c_gsum"], u.count(1, 1))
                    dve.reciprocal(ginv[:], gsum[:]).then_inc(s["c_ginv"], 1)
                    wait(dve, s["c_ginv"], u.count(1, 1))
                    dve.tensor_tensor(gate[u.parity][:], eg[:], ginv[:].unsqueeze(2).to_broadcast([128, TC, E]),
                                      ALU.mult).then_inc(s["c_pr"], 1)
                if T == 117:
                    wait(dve, s["c_b2"], u.count(1, 1))
                    wait(dve, s["c_x1t"], u.count(1, 1))
                    dve.tensor_tensor(yacc[u.parity][:], misc[:], x1t[:], ALU.add).then_inc(s["c_y0"], 1)
                if T == 21 - TICKS:
                    if i0 == -1:
                        dve.wait_ge(s["ld_x0"], 16)
                    elif i0 < MID_FIRST:
                        wait(dve, s["ld_x"], 16 * (B - 1))
                    else:
                        wait(dve, s["m_x"], u.n - (B - 2))
                    moments("f", u.n, lambda c: slot(u.n, c, 1))
                if T == 23 - TICKS:
                    wait(dve, s["f_xT"], u.count(1, 0))
                    normalise("f", u.n, f_xn, lambda c: slot(u.n, c, 1), "f_xn")
                if T == 26 - TICKS:
                    wait(dve, s["f_xh"], u.count(1, 1))
                    dve.tensor_tensor(xl[:, 1:S + 1], misc[:], xh[:, 1:S + 1].bitcast(F32), ALU.subtract)\
                        .then_inc(s["f_xl"], 1)
                if T == 36 - TICKS:
                    wait(dve, s["f_ch"], u.count(1, 1))
                    dve.scalar_tensor_tensor(out=cl[u.parity][:], in0=misc[:], scalar=col(V_CONV),
                                             in1=ch[u.parity][:].bitcast(F32), op0=ALU.add, op1=ALU.subtract)\
                        .then_inc(s["f_cl"], 1)
                for k, at, bias in ((0, 38 - TICKS, V_BQ), (1, 42 - TICKS, V_BK)):
                    if T == at:
                        wait(dve, s["f_p1"], u.count(2, k + 1))
                        wait(dve, s["f_p3"], u.count(2, k))
                        dve.scalar_tensor_tensor(out=rest[:], in0=misc[:], scalar=col(bias),
                                                 in1=parts[k][:, 0, :], op0=ALU.add, op1=ALU.subtract)\
                            .then_inc(s["f_r1"], 1)
                    if T == at + 1:
                        wait(dve, s["f_p2"], u.count(2, k + 1))
                        dve.tensor_tensor(parts[k][:, 2, :], rest[:], parts[k][:, 1, :], ALU.subtract)\
                            .then_inc(s["f_p3"], 1)
                if T == 55 - TICKS:
                    wait(dve, s["f_v"], u.count(1, 1))
                    wait(dve, s["a_pv"], (u.n - 1) * 16)
                    dve.tensor_tensor(V[u.parity][:, :, :, 0:DH],
                                      misc[:].rearrange("p (c h d) -> p c h d", c=TC, h=H),
                                      bv_b[:].rearrange("p (h d) -> p h d", h=H).unsqueeze(1)
                                      .to_broadcast([128, TC, H, DH]), ALU.add).then_inc(s["f_vs"], 1)

            def by_offset(ap):
                return ap.rearrange("p (n s r) -> p n r s", n=NSG, r=DIL)

            def over_steps(v):
                return v[:].unsqueeze(3).to_broadcast([128, NSG, DIL, SEG // DIL])

            def mid(t, b, i, i0):
                if t == 0:
                    wait(dve, s["e_x"], b.count(1, 1))
                    moments("m", b.n, lambda c: slot(b.n, c, 1))
                if t == 2:
                    normalise("m", b.n, m_xn, lambda c: slot(b.n, c, 1), "m_xn")
                if t == 5:
                    wait(dve, s["m_xh"], b.count(1, 1))
                    dve.tensor_tensor(mxl[:], misc[:], mxh[:].bitcast(F32), ALU.subtract).then_inc(s["m_xl"], 1)
                if t == 9:
                    wait(dve, s["m_k"], b.count(1, 1))
                    wait(dve, s["m_mq"], b.count(1, 1))
                    dve.scalar_tensor_tensor(out=mq[:], in0=misc[:], scalar=col(V_MBK), in1=mq[:],
                                             op0=ALU.add, op1=ALU.mult).then_inc(s["m_qk"], 1)
                if t == 14:
                    wait(dve, s["m_s"], b.count(1, 1))
                    dve.tensor_reduce(mmax[:], by_offset(misc[:]), AX.X, ALU.max).then_inc(s["m_max"], 1)
                    wait(dve, s["m_max"], b.count(1, 1))
                    dve.tensor_tensor(by_offset(m_xn[:]), by_offset(misc[:]), over_steps(mmax), ALU.subtract)\
                        .then_inc(s["m_sc"], 1)
                if t == 16:
                    wait(dve, s["m_ex"], b.count(1, 1))
                    dve.tensor_reduce(msum[:], by_offset(m_xn[:]), AX.X, ALU.add).then_inc(s["m_sum"], 1)
                    wait(dve, s["m_sum"], b.count(1, 1))
                    dve.reciprocal(minv[:], msum[:]).then_inc(s["m_inv"], 1)
                    wait(dve, s["m_inv"], b.count(1, 1))
                    wait(dve, s["mask_ready"], 1)
                    dve.tensor_tensor(mwt[:], minv[:], dil_mask[:].unsqueeze(1).to_broadcast([128, NSG, DIL]),
                                      ALU.mult).then_inc(s["m_wt"], 1)
                if t == 18:
                    wait(dve, s["m_wt"], b.count(1, 1))
                    dve.tensor_tensor(by_offset(m_xn[:]), by_offset(m_xn[:]), over_steps(mwt), ALU.mult)\
                        .then_inc(s["m_w"], 1)
                if t == 21:
                    wait(dve, s["m_v"], b.count(1, 1))
                    wait(dve, s["m_w"], b.count(1, 1))
                    dve.scalar_tensor_tensor(out=m_xn[:], in0=misc[:], scalar=col(V_MBV), in1=m_xn[:],
                                             op0=ALU.add, op1=ALU.mult).then_inc(s["m_o"], 1)
                if t == 23:
                    wait(dve, s["m_out"], b.count(1, 1))
                    dve.tensor_tensor(mq[:].rearrange("p (c d) -> p c d", c=TC),
                                      misc[:].rearrange("p (c d) -> p c d", c=TC),
                                      mbo_b[:].unsqueeze(1).to_broadcast([128, TC, D]), ALU.add)\
                        .then_inc(s["m_t"], 1)
                if t == 24:
                    wait(dve, s["m_t"], b.count(1, 1))
                    dve.tensor_tensor(slot(b.n), slot(b.n), mq[:], ALU.add).then_inc(s["m_x"], 1)

            def iteration(i, p, i0):
                if i0 == 0:
                    split_w1()
                walk(i, p, i0, tick, mid)

            run(dve, iteration)

        @block.tensor
        def _(pe):
            def three(dst, hi, lo, rhi, rlo, start=True, stop=True):
                pe.matmul(dst, hi, rhi, start=start, stop=False)
                pe.matmul(dst, hi, rlo, start=False, stop=False)
                return pe.matmul(dst, lo, rhi, start=False, stop=stop)

            pe.wait_ge(s["ident_ready"], 1)
            pe.wait_ge(s["ld_vec"], 16 * (E + 8))
            pe.transpose(misc[:, 0:NV], vec_rows, ident[0:NV, 0:NV]).then_inc(s["set_vT"], 1)
            pe.wait_ge(s["set_cols"], 1)
            pe.wait_ge(s["ld_conv"], 16)
            for j in range(3):
                last = pe.transpose(misc[:, j * D:(j + 1) * D], conv_raw[:, :, j], ident[:])
            last.then_inc(s["set_cT"], 1)
            pe.wait_ge(s["set_cl"], 1)
            pe.wait_ge(s["ld_qkv"], 16)
            for j in range(3):
                last = pe.transpose(misc[:, j * D:(j + 1) * D], wqkv_raw[:, j, :], ident[:])
            last.then_inc(s["set_qT"], 1)
            pe.wait_ge(s["set_ql"], 1)
            pe.wait_ge(s["ld_wo"], 16)
            pe.transpose(misc[:, 0:D], wo_raw, ident[:]).then_inc(s["set_oT"], 1)
            pe.wait_ge(s["set_ml"], 1)
            pe.wait_ge(s["ld_small"], 48)

            def tick(T, u, t, i, i0):
                p = u.parity
                if T == 26 - TICKS:
                    wait_misc(pe, t, i, i0)
                    wait(pe, s["f_xn"], u.count(1, 1))
                    for c in range(TC):
                        last = pe.transpose(chunk(misc, c), chunk(f_xn, c), ident[:])
                    last.then_inc(s["f_xT"], 1)
                if T == 36 - TICKS:
                    wait_misc(pe, t, i, i0)
                    wait(pe, s["f_xl"], u.count(1, 1))
                    for j in range(3):
                        last = three(misc[:], cwh[:, j, :], cwl[:, j, :], xh[:, j:j + S], xl[:, j:j + S],
                                     start=(j == 0), stop=(j == 2))
                    last.then_inc(s["f_conv"], 1)
                for k, at in ((0, 38 - TICKS), (1, 42 - TICKS)):
                    if T == at:
                        wait_misc(pe, t, i, i0)
                        wait(pe, s["f_cl"], u.count(1, 1))
                        three(misc[:], qkh[:, k, :], qkl[:, k, :], ch[p][:], cl[p][:]).then_inc(s["f_qk"], 1)
                if T == 55 - TICKS:
                    wait_misc(pe, t, i, i0)
                    for c in range(TC):
                        pe.matmul(chunk(misc, c), chunk(ch[p], c).bitcast(F32), wvT[:], start=True, stop=False)
                        last = pe.matmul(chunk(misc, c), chunk(cl[p], c).bitcast(F32), wvT[:], start=False,
                                         stop=True)
                    last.then_inc(s["f_v"], 1)
                if T in NM_AT:
                    g = NM_AT[T]
                    wait_misc(pe, t, i, i0)
                    wait(pe, s["a_max"], u.count(64, 16 * g + 16))
                    pe.transpose(misc[0:HG * TC, 0:128], negmax[:, g % 2, :], ident[:]).then_inc(s["a_nmT"], 1)
                if T in CTX_AT:
                    g = CTX_AT[T]
                    wait_misc(pe, t, i, i0)
                    wait(pe, s["a_ctx"], u.count(4, g + 1))
                    for c in range(TC):
                        last = pe.transpose(chunk(misc, c), chunk(ctxT, c), ident[:])
                    last.then_inc(s["a_ctxT"], 1)
                if T == 95:
                    wait_misc(pe, t, i, i0)
                    wait(pe, s["a_norm"], u.count(4, 4))
                    for c in range(TC):
                        last = pe.transpose(chunk(misc, c), ctxs[:, c, :, :].rearrange("p h d -> p (h d)"), ident[:])
                    last.then_inc(s["c_cT"], 1)
                if T == 98:
                    wait_misc(pe, t, i, i0)
                    wait(pe, s["c_cTs"], u.count(1, 1))
                    for c in range(TC):
                        pe.matmul(chunk(misc, c), chunk(ctxT, c), woT[:], start=True, stop=False)
                        pe.matmul(chunk(misc, c), chunk(ch[p], c).bitcast(F32), ident[:], start=False, stop=False)
                        last = pe.matmul(chunk(misc, c), chunk(cl[p], c).bitcast(F32), ident[:], start=False,
                                         stop=True)
                    last.then_inc(s["c_x1"], 1)
                if T == 104:
                    wait_misc(pe, t, i, i0)
                    wait(pe, s["c_xn"], u.count(1, 1))
                    for c in range(TC):
                        last = pe.transpose(chunk(misc, c), chunk(x1n, c), ident[:])
                    last.then_inc(s["c_xnT"], 1)
                if T == 110:
                    wait_misc(pe, t, i, i0)
                    for c in range(TC):
                        last = pe.matmul(misc[:, c * E:(c + 1) * E], chunk(x1f, c), gws[:], start=True, stop=True)
                    last.then_inc(s["c_gate"], 1)
                if T == 115:
                    wait_misc(pe, t, i, i0)
                    wait(pe, s["c_pr"], u.count(1, 1))
                    for c in range(TC):
                        last = pe.transpose(misc[0:E, c * 128:(c + 1) * 128], gate[p][:, c, :], ident[:])
                    last.then_inc(s["c_prT"], 1)
                if T == 117:
                    wait_misc(pe, t, i, i0)
                    for c in range(TC):
                        last = pe.matmul(chunk(misc, c), chunk(gateT, c), b2s[:], start=True, stop=True)
                    last.then_inc(s["c_b2"], 1)
                if P2_AT <= T < P2_AT + 64:
                    k = T - P2_AT
                    n, j = divmod(k, HG)
                    g, kc = divmod(n, TC)
                    if k % 16 == 0:
                        wait(pe, s["a_m_in"], u.count(48 * G, 48 * (g + 1)))
                    wait(pe, s["a_exp"], u.count(64, k - 1))
                    pe.matmul(score2[k % 2][:], Kp[:, g * HG + j, kc * 128:(kc + 1) * 128],
                              Qp[:, g * HG + j, :], start=True, stop=True).then_inc(s["a_s2"], 1)
                if 0 <= T < 64:
                    h, qc = divmod(T, TC)
                    if T % 16 == 0:
                        wait(pe, s["pack_in"], u.count(192 * G, 192 * (h // HG + 1)))
                    wait(pe, s["a_max"], u.count(64, T - 1))
                    pe.matmul(score1[T % 2][:], Qp[0:SCORE_ROWS, h, qc * 128:(qc + 1) * 128],
                              Kp[0:SCORE_ROWS, h, :], start=True, stop=True).then_inc(s["a_s1"], 1)
                k = T - P2_AT - PV_LAG
                if 0 <= k < 64 and k % HG == 0:
                    n = k // HG
                    g, kc = divmod(n, TC)
                    wait(pe, s["a_exp"], u.count(64, 4 * n + 4))
                    if n == 0:
                        wait(pe, s["f_vs"], u.count(1, 1))
                        wait(pe, s["zero_v"], 1)
                    if kc == 0:
                        wait(pe, s["a_ctx"], u.count(4, g))
                    for j in range(HG):
                        last = pe.matmul(ctx_ps[32 * j:32 * j + DH + 1, :], V[p][:, kc, g * HG + j, :],
                                         probs[:, n % 2, j, :], start=(kc == 0), stop=(kc == TC - 1))
                    last.then_inc(s["a_pv"], 1)
                m = T - EXPERTS_AT
                if 0 <= m < 64 and m % 2 == 0:
                    n = m // 2
                    if n == 0:
                        wait(pe, s["c_x1l"], u.count(1, 1))
                    if i0 < 2:
                        wait(pe, s["set_w1l"], E)
                    wait(pe, s["h_relu"], u.count(32, n))
                    w = slice(n * 128, (n + 1) * 128)
                    three(hid_ps[:], w1h[:, w], w1l[:, w], x1h[p][:], x1l[p][:]).then_inc(s["h_mm"], 1)
                m = T - EXPERTS_AT - 8
                if 0 <= m < 64 and m % 2 == 1:
                    e, c = divmod(m // 2, TC)
                    if c == 0:
                        wait(pe, s["h_relu"], u.count(32, 4 * e + 4))
                        wait(pe, s["y_acc"], u.count(8, e))
                        if i0 < 2:
                            wait(pe, s["ld_w2"], 16 * E)
                    for f in range(FC):
                        last = pe.matmul(chunk(y_ps, c), chunk(hid[:, e % 2, f, :], c), w2s[:, e * FC + f, :],
                                         start=(f == 0), stop=(f == FC - 1))
                    if c == TC - 1:
                        last.then_inc(s["y_mm"], 1)

            def mid(t, b, i, i0):
                if t == 5:
                    wait_misc(pe, t, i, i0)
                    wait(pe, s["m_xn"], b.count(1, 1))
                    for c in range(TC):
                        last = pe.transpose(chunk(misc, c), chunk(m_xn, c), ident[:])
                    last.then_inc(s["m_xT"], 1)
                for k, at, done in ((0, 7, "m_q"), (1, 9, "m_k"), (2, 21, "m_v")):
                    if t == at:
                        wait_misc(pe, t, i, i0)
                        wait(pe, s["m_xl"], b.count(1, 1))
                        three(misc[:], mwh[:, k, :], mwl[:, k, :], mxh[:], mxl[:]).then_inc(s[done], 1)
                if t == 14:
                    wait_misc(pe, t, i, i0)
                    wait(pe, s["m_qk"], b.count(1, 1))
                    pe.matmul(misc[:], heads8[:], mq[:], start=True, stop=True).then_inc(s["m_s"], 1)
                if t == 23:
                    wait_misc(pe, t, i, i0)
                    wait(pe, s["m_o"], b.count(1, 1))
                    for c in range(TC):
                        last = pe.matmul(chunk(misc, c), chunk(m_xn, c), mwo[:], start=True, stop=True)
                    last.then_inc(s["m_out"], 1)

            run(pe, lambda i, p, i0: walk(i, p, i0, tick, mid))


_INS = ["L0_attn_x", "L0_attn_Wq", "L0_attn_bq", "L0_attn_Wk", "L0_attn_bk", "L0_attn_Wv", "L0_attn_bv",
        "L0_attn_Wo", "L0_attn_bo", "L0_ffn_conv_w", "L0_ffn_conv_b", "L0_ffn_wqkv", "L0_ffn_bqkv", "L0_ffn_wo",
        "L0_ffn_bo", "L0_ffn_ln1_g", "L0_ffn_ln1_b", "L0_ffn_gate_w", "L0_ffn_gate_b", "L0_ffn_w1", "L0_ffn_b1",
        "L0_ffn_w2", "L0_ffn_b2", "L0_ffn_ln2_g", "L0_ffn_ln2_b"]


def kernel(**inputs):
    import concourse.bacc as bacc
    from concourse.bass_utils import run_bass_kernel_spmd

    nc = bacc.Bacc("TRN2", target_bir_lowering=False, num_devices=1)
    arrays, args = {}, []
    for name in _INS:
        a = np.ascontiguousarray(inputs[name])
        arrays[f"in_{name}"] = a
        args.append(nc.dram_tensor(f"in_{name}", a.shape, mybir.dt.from_np(a.dtype), kind="ExternalInput").ap())
    args.append(nc.dram_tensor("out", (B, S, D), F32, kind="ExternalOutput").ap())
    macaron(nc, *args)
    return run_bass_kernel_spmd(nc, [arrays], core_ids=[0]).results[0]["out"]
```

```python
from contextlib import ExitStack

import numpy as np

import concourse.bass as bass
from concourse import mybir

ALU = mybir.AluOpType
ACT = mybir.ActivationFunctionType
AX = mybir.AxisListType
F32 = mybir.dt.float32
F32R = mybir.dt.float32r
BF16 = mybir.dt.bfloat16

B, S, D = 8, 512, 128
H, DH = 16, 8
E, FF = 8, 512
TC = S // 128
FC = FF // 128
G, HG = 4, 4
SEG, DIL = 64, 4
EPS = 1e-5
SCALE = float(DH) ** -0.5
UNITS = 2 * B

PART_OF_ROW = ((0, 0, 0, 1, 1, 2), (0, 1, 2, 0, 1, 0))
PAIRS = len(PART_OF_ROW[0])
SCORE_ROWS = 96
MAX_ROW = 96
TWO_ONES = float(np.array([0x3F803F80], np.uint32).view(np.float32)[0])

TICKS = 64
P2_AT = 24
PV_LAG = 5
EXPERTS_AT = 112
DOWN_LAG = 6
RING = 4
GATE_RING = 4
MID_FIRST = 6


class Unit:

    def __init__(self, number, parity):
        self.n, self.parity = number, parity

    def count(self, per_unit, k):
        return per_unit * self.n + k


def wait(eng, sem, value):
    if isinstance(value, int) and value <= 0:
        return
    eng.wait_ge(sem, value)


def macaron(nc, x, Wq, bq, Wk, bk, Wv, bv, Wo, bo, conv_w, conv_b, wqkv, bqkv, wo, bo2, ln1_g, ln1_b,
            gate_w, gate_b, w1, b1, w2, b2, ln2_g, ln2_b, out):
    with ExitStack() as ctx:
        def sb(name, shape, dt=F32):
            return ctx.enter_context(nc.sbuf_tensor(name, shape, dt))

        def psum(name):
            return ctx.enter_context(nc.psum_tensor(name, [128, 512], F32))

        def sem(name):
            return ctx.enter_context(nc.semaphore(name))

        score1 = [psum("score1a"), psum("score1b")]
        score2 = [psum("score2a"), psum("score2b")]
        ctx_ps = psum("ctx_ps")
        hid_ps = psum("hid_ps")
        y_ps = psum("y_ps")
        misc = psum("misc")

        w1h, w1l = sb("w1h", [128, E * FF], F32R), sb("w1l", [128, E * FF], F32R)
        w2h, w2l = sb("w2h", [128, E * FC, D], F32R), sb("w2l", [128, E * FC, D], F32R)
        gws = sb("gws", [128, E])
        cwh, cwl = sb("cwh", [128, 3, D], F32R), sb("cwl", [128, 3, D], F32R)
        qkh, qkl = sb("qkh", [128, 2, D], F32R), sb("qkl", [128, 2, D], F32R)
        wvT, woT = sb("wvT", [128, D]), sb("woT", [128, D])
        mwh, mwl = sb("mwh", [128, 3, D], F32R), sb("mwl", [128, 3, D], F32R)
        mwo = sb("mwo", [128, D])
        NV = E * FC + 8 + E
        cols = sb("cols", [128, NV])
        (V_CONV, V_BQ, V_BK, V_G1, V_B1, V_MBQ, V_MBK, V_MBV) = range(E * FC, E * FC + 8)
        V_B2 = E * FC + 8
        names = ["bv_b", "bo_b", "g2_b", "b2_b", "mbo_b"]
        bv_b, bo_b, g2_b, b2_b, mbo_b = (sb(n, [128, D]) for n in names)
        gb_b = sb("gb_b", [128, E])
        ident, heads8 = sb("ident", [128, 128]), sb("heads8", [128, 128])
        dil_mask = sb("dil_mask", [128, DIL])
        minus_half, eps_t = sb("minus_half", [128, TC]), sb("eps_t", [128, TC])
        resid = sb("resid", [128, S])
        f_xn = sb("f_xn", [128, S])
        xh, xl = sb("xh", [128, S + 2], F32R), sb("xl", [128, S + 2], F32R)
        ch, cl = sb("ch", [128, S], F32R), sb("cl", [128, S], F32R)
        conv = [sb(f"conv{p}", [128, S]) for p in range(2)]
        parts = [sb("q_parts", [128, 3, S], BF16), sb("k_parts", [128, 3, S], BF16)]
        rest = sb("rest", [128, S])
        Qp, Kp = sb("Qp", [128, H, S], BF16), sb("Kp", [128, H, S], BF16)
        V = [sb(f"V{p}", [128, TC, H, DH + 1]) for p in range(2)]
        negmax = sb("negmax", [128, 2, HG * TC])
        m_parts, m_rest = sb("m_parts", [HG * TC, 3, 128], BF16), sb("m_rest", [HG * TC, 128])
        probs = sb("probs", [128, 2, HG, S])
        ctxT = sb("ctxT", [128, S])
        rden = sb("rden", [128, TC, HG])
        ctxs = sb("ctxs", [128, TC, H, DH])
        x1n = sb("x1n", [128, S])
        x1h, x1l = sb("x1h", [128, S], F32R), sb("x1l", [128, S], F32R)
        lg, lg2, eg = sb("lg", [128, TC, E]), sb("lg2", [128, TC, E]), sb("eg", [128, TC, E])
        gmax, gsum, ginv = sb("gmax", [128, TC]), sb("gsum", [128, TC]), sb("ginv", [128, TC])
        gate = [sb(f"gate{p}", [128, TC, E]) for p in range(2)]
        gateT = sb("gateT", [E, S])
        hid = sb("hid", [128, 2, S])
        hidh, hidl = sb("hidh", [128, RING, S], F32R), sb("hidl", [128, RING, S], F32R)
        gate_b128 = sb("gate_b128", [128, GATE_RING, S])
        gated = sb("gated", [128, S])
        yacc = [sb(f"yacc{p}", [128, S]) for p in range(2)]
        zn = x1n
        m_xn = sb("m_xn", [128, S])
        mxh, mxl = xh[:, 1:S + 1], xl[:, 1:S + 1]
        mq = rest
        NSG = S // SEG
        mmax, msum, minv, mwt = (sb(n, [128, NSG, DIL]) for n in ("mmax", "msum", "minv", "mwt"))
        ln = {k: (sb(f"{k}_st", [128, TC, 6]), sb(f"{k}_mv", [128, TC, 2]), sb(f"{k}_ve", [128, TC]),
                  sb(f"{k}_rs", [128, TC])) for k in ("f", "c", "e", "m")}
        turned_vec, turned_conv, turned_qkv, turned_wo = score1[0], score1[1], score2[0], score2[1]
        stage = probs[:].rearrange("p a j q -> p (a j q)")
        conv_raw = stage[:, 0:3 * D].rearrange("p (i j) -> p i j", j=3)
        wqkv_raw = stage[:, 3 * D:6 * D].rearrange("p (j i) -> p j i", j=3)
        mws = stage[:, 6 * D:9 * D].rearrange("p (j i) -> p j i", j=3)
        wo_raw = stage[:, 9 * D:10 * D]
        vec_rows = stage[0:NV, 10 * D:11 * D]
        dram = [nc.dram_tensor(f"{n}_dram", [3, H, DH, S], BF16).ap() for n in ("q_parts", "k_parts")]
        stream = nc.dram_tensor("stream_dram", [B, S, D], F32).ap()
        gate_dram = nc.dram_tensor("gate_dram", [E, S], F32).ap()

        s = {}
        for n in """
            ld_x ld_vec ld_small ld_conv ld_qkv ld_wo ld_mid ld_bc
            zero_v k_zero pack_zero ident0 ident_ready held_dve held_sp heads0 heads1 heads_ready mask_ready g2_half
            set_vT set_cols set_cT set_ch set_cl set_qT set_qh set_ql set_oT set_mh set_ml
            set_wh set_wl
            f_bn f_mv f_ve f_rs c_bn c_mv c_ve c_rs e_bn e_mv e_ve e_rs m_bn m_mv m_ve m_rs
            f_xn f_xT f_xh f_xl f_conv f_c f_ch f_cl f_qk f_p1 f_r1 f_p2 f_p3 f_v f_vs parts_out pack_in
            a_s1 a_max a_nmT a_m1 a_r1 a_m2 a_m3 a_m_in a_s2 a_exp a_pv a_ctx a_ctxT a_rden a_norm
            c_cT c_cTs c_x1 c_x1p c_xn c_xnT c_x1h c_x1f c_x1l gate_out gate_in
            c_gate f_in e_in e_stored m_in m_in2 m_stored c_lg c_gmax c_lg2 c_eg c_gsum c_ginv c_pr c_prT c_prTs 
            h_mm h_hi h_full h_lo h_lo_last y_mm y_gated y_acc
            e_T e_t e_zn e_zg e_zb e_x
            m_xn m_xT m_xh m_xl m_q m_mq m_k m_qk m_s m_max m_sc m_ex m_sum m_inv m_wt m_w m_v m_o m_out m_t
            m_x
        """.split():
            assert n not in s, n
            s[n] = sem(n)

        def col(k):
            return cols[:, k:k + 1]

        def chunk(ap, c):
            return ap[:, c * 128:(c + 1) * 128]

        def rows_of(dram, b):
            at = dram[b:b + 1] if isinstance(b, int) else dram[bass.ds(b, 1)]
            return at.rearrange("a (c p) d -> p (a c) d", p=128)

        def chunks(tile):
            return tile[:].rearrange("p (c d) -> p c d", c=TC)

        s["ld_w"] = [sem(f"ld_w{k}") for k in range(GATE_RING)]

        LAST_UNIT = UNITS - 1
        misc_uses = sorted(
            [(17 + 16 * g - TICKS * b, b, "a_m3r", 4, g + 1) for g, b in ((0, 0), (1, 0), (2, 0), (3, 1))]
            + [(44 + 16 * g - TICKS * b, b, "a_norm", 4, g + 1) for g, b in ((0, 0), (1, 0), (2, 1), (3, 1))]
            + [(31, 1, "c_cTs", 1, 1), (34, 1, "c_x1p", 1, 1), (46, 1, "c_x1h", 1, 1), (50, 1, "c_lg", 1, 1),
               (54, 1, "c_prTs", 1, 1), (55, 2, "e_t", 1, 1)]
            + [(26, -1, "f_xl", 1, 1), (36, -1, "f_cl", 1, 1), (38, -1, "f_r1", 2, 1), (41, -1, "f_r1", 2, 2),
               (58, -1, "f_vs", 1, 1)]
            + [(8, "mid", "m_xl", 1, 1), (11, "mid", "m_mq", 1, 1), (14, "mid", "m_qk", 1, 1),
               (20, "mid", "m_sc", 1, 1), (24, "mid", "m_o", 1, 1), (29, "mid", "m_t", 1, 1)],
            key=lambda use: use[0])
        assert len({use[0] for use in misc_uses}) == len(misc_uses)

        def in_iteration(i0, back):
            if back == "mid":
                return MID_FIRST <= i0 < MID_FIRST + B
            return 0 <= i0 - back <= LAST_UNIT

        def wait_misc(pe, tick, i, i0):
            before = [(t, b, n, per, k, 0) for t, b, n, per, k in misc_uses if t < tick]
            earlier = [(t, b, n, per, k, 1) for t, b, n, per, k in misc_uses]
            for t, b, n, per, k, ago in reversed(earlier + before):
                if in_iteration(i0 - ago, b):
                    u = i - ago - (MID_FIRST if b == "mid" else b)
                    name = "a_r1" if n == "a_m3r" else n
                    wait(pe, s[name], per * u + k)
                    return

        def run(eng, iteration):
            for i in (-1, 0, 1):
                iteration(i, i % 2, i)
            for a, b in ((2, MID_FIRST), (MID_FIRST, MID_FIRST + B)):
                with eng.Fori(a, b, 2) as r:
                    iteration(r, 0, a + 2)
                    iteration(r + 1, 1, a + 3)
            for i in (14, 15, 16, 17):
                iteration(i, i % 2, i)

        def walk(i, parity, i0, unit_tick, mid_tick=None):
            for t in range(TICKS):
                if mid_tick and in_iteration(i0, "mid"):
                    mid_tick(t, Unit(i - MID_FIRST, parity), i, i0)
                for back in (2, 1, 0, -1):
                    if in_iteration(i0, back):
                        unit_tick(t + TICKS * back, Unit(i - back, (parity - back) % 2), t, i, i0)

        def staged(k):
            return gate_b128[:, k % GATE_RING, :], s["ld_w"][k % GATE_RING], 16 * (k // GATE_RING + 1)

        def split_of(k):
            if k < E:
                return [w[:, k * FF:(k + 1) * FF] for w in (w1h, w1l)]
            return [w[:, (k - E) * FC:(k - E + 1) * FC, :].rearrange("p f d -> p (f d)") for w in (w2h, w2l)]

        def is_last(T, t, i0):
            return i0 - (T - t) // TICKS == LAST_UNIT

        def wait_lo(eng, u, k, last):
            if last and k > 0:
                wait(eng, s["h_lo_last"], k)
            else:
                wait(eng, s["h_lo"], u.count(32, k))

        SPLIT_EVERY = TICKS // (2 * E)

        NM_AT = {17 + 16 * g: g for g in range(G)}
        CTX_AT = {44 + 16 * g: g for g in range(G)}
        LOADS_AT = {-16: 0, -6: 1, 9: 2, 25: 3}

        block = ctx.enter_context(nc.Block())

        @block.sync
        def _(sp):
            def load(dst, src, name):
                sp.dma_start(dst, src).then_inc(s[name], 16)

            def row(v):
                return v.rearrange("(a n) -> a n", a=1)

            sp.dma_start(chunks(f_xn), rows_of(x, 0)).then_inc(s["f_in"], 16)
            load(conv_raw, conv_w, "ld_conv")
            for r in range(0, E):
                load(vec_rows[r * FC:(r + 1) * FC, :], b1[r].rearrange("(f p) -> f p", p=128), "ld_vec")
            load(vec_rows[V_CONV:V_CONV + 1, :], row(conv_b), "ld_vec")
            load(vec_rows[V_BQ:V_BQ + 2, :], bqkv[0:2 * D].rearrange("(a n) -> a n", a=2), "ld_vec")
            for k, v in ((V_G1, ln1_g), (V_B1, ln1_b), (V_MBQ, bq), (V_MBK, bk), (V_MBV, bv))[0:5]:
                load(vec_rows[k:k + 1, :], row(v), "ld_vec")
            load(vec_rows[V_B2:V_B2 + E, :], b2, "ld_vec")
            load(wqkv_raw, wqkv.rearrange("(j o) i -> o j i", j=3), "ld_qkv")
            load(wo_raw, wo, "ld_wo")
            for k, v in enumerate((Wq, Wk, Wv)):
                load(mws[:, k, :], v, "ld_mid")
            for dst, v in ((bv_b, bqkv[2 * D:3 * D]), (bo_b, bo2), (g2_b, ln2_g),
                           (b2_b, ln2_b), (mbo_b, bo)):
                load(dst[:], v.partition_broadcast(128), "ld_bc")
            load(gb_b[:], gate_b.partition_broadcast(128), "ld_bc")
            load(mwo[:], Wo, "ld_small")
            load(gws[:], gate_w, "ld_small")
            load(stream[B // 2:], x[B // 2:], "ld_x")
            def wait_sp(sem, value):
                wait(sp, sem, value)
                sp.sem_inc(s["held_sp"], 1)

            def tick(T, u, t, i, i0):
                for k, at in ((0, 40 - TICKS), (1, 43 - TICKS)):
                    if T == at:
                        wait_sp(s["f_p3"], u.count(2, k + 1))
                        wait_sp(s["pack_in"], u.count(192 * G, 0))
                        sp.dma_start(dram[k].rearrange("a h d q -> (h d) a q"), parts[k][:]).then_inc(s["parts_out"], 16)
                if T in LOADS_AT:
                    g = LOADS_AT[T]
                    wait_sp(s["parts_out"], u.count(32, 32))
                    wait_sp(s["a_s2"], (u.n - 1) * 64 + 16 * g + 16)
                    wait_sp(s["pack_zero"], 2)
                    wait_sp(s["pack_in"], u.count(192 * G, 192 * g))
                    hs = slice(g * HG, (g + 1) * HG)
                    for k, packed in ((0, Qp), (1, Kp)):
                        for row, part in enumerate(PART_OF_ROW[k]):
                            sp.dma_start(packed[row * DH:(row + 1) * DH, hs, :],
                                         dram[k][part, hs, :, :].rearrange("h d q -> d h q"))\
                                .then_inc(s["pack_in"], 16)
                if T - 2 in NM_AT:
                    g = NM_AT[T - 2]
                    wait_sp(s["a_m3"], u.count(4, g + 1))
                    wait_sp(s["pack_zero"], 2)
                    for part in range(3):
                        sp.dma_start(Qp[MAX_ROW + part:MAX_ROW + part + 1, g * HG:(g + 1) * HG, :],
                                     m_parts[:, part, :]).then_inc(s["a_m_in"], 16)
                if T == 119:
                    wait_sp(s["c_prTs"], u.count(1, 1))
                    wait_sp(s["gate_in"], u.count(32, 0))
                    sp.dma_start(gate_dram, gateT[:]).then_inc(s["gate_out"], 16)
                for half, at in ((0, 120), (1, 151)):
                    if T == at:
                        es = slice(half * GATE_RING, (half + 1) * GATE_RING)
                        wait_sp(s["gate_out"], u.count(16, 16))
                        wait_sp(s["y_gated"], u.count(8, half * GATE_RING))
                        if i0 < 2:
                            sp.wait_ge(s["set_wl"], 2 * E)
                        wait_sp(s["gate_in"], u.count(32, 16 * half))
                        sp.dma_start(gate_b128[:], gate_dram[es].partition_broadcast(128))\
                            .then_inc(s["gate_in"], 16)
                if T == 18 - TICKS and i0 >= 0:
                    wait_sp(s["f_xT"], u.count(1, 0))
                    if i0 < MID_FIRST:
                        sp.dma_start(chunks(f_xn), rows_of(x, u.n % B)).then_inc(s["f_in"], 16)
                    else:
                        sp.wait_ge(s["ld_x"], 16)
                        wait_sp(s["m_stored"], (u.n - (B - 2)) * 16)
                        sp.dma_start(chunks(f_xn), rows_of(stream, u.n % B)).then_inc(s["f_in"], 16)
                if T == 180:
                    wait_sp(s["e_stored"], u.count(16, 0))
                    if i0 > MID_FIRST:
                        wait_sp(s["m_stored"], ended_mids(i, i0) * 16 + 16)
                    src = rows_of(x, u.n % B) if i0 < MID_FIRST else rows_of(stream, u.n % B)
                    sp.dma_start(chunks(resid), src).then_inc(s["e_in"], 16)
                if T == 191:
                    wait_sp(s["e_x"], u.count(1, 1))
                    sp.dma_start(rows_of(out, u.n % B), chunks(resid)).then_inc(s["e_stored"], 16)

            def ended_mids(i, i0):
                return i - MID_FIRST + 1 if i0 < MID_FIRST + B else B

            def mid(t, b, i, i0):
                if t == 0:
                    wait_sp(s["e_stored"], (b.n + 1) * 16)
                    wait_sp(s["m_out"], b.count(1, 0))
                    sp.dma_start(chunks(m_xn), rows_of(out, b.n % B)).then_inc(s["m_in"], 16)
                if t == 20:
                    wait_sp(s["e_stored"], (i - 2) * 16)
                    sp.dma_start(chunks(resid), rows_of(out, b.n % B)).then_inc(s["m_in2"], 16)
                if t == 33:
                    wait_sp(s["m_x"], b.count(1, 1))
                    sp.dma_start(rows_of(stream, b.n % B), chunks(resid)).then_inc(s["m_stored"], 16)

            sp.sem_inc(s["m_stored"], 16)
            run(sp, lambda i, p, i0: walk(i, p, i0, tick, mid))
            sp.wait_ge(s["e_stored"], 16 * UNITS)

        @block.gpsimd
        def _(pool):
            pool.memset(ident[:], 0.0).then_inc(s["ident0"], 1)
            pool.wait_ge(s["ident0"], 1)
            pool.affine_select(out=ident[:], in_=ident[:], compare_op=ALU.not_equal, fill=1.0, base=0,
                               pattern=[[-1, 128]], channel_multiplier=1).then_inc(s["ident_ready"], 1)
            pool.memset(Qp[:].bitcast(F32), 0.0).then_inc(s["pack_zero"], 1)
            pool.memset(minus_half[:], -0.5).then_inc(s["heads0"], 1)
            pool.memset(eps_t[:], EPS).then_inc(s["heads0"], 1)
            pool.memset(heads8[:], 1.0).then_inc(s["heads0"], 1)
            pool.wait_ge(s["heads0"], 3)
            blocks = heads8[:].rearrange("p (h d) -> p h d", d=DH)
            pool.affine_select(out=blocks, in_=blocks, compare_op=ALU.is_ge, fill=0.0, base=0,
                               pattern=[[-DH, H], [0, DH]], channel_multiplier=1).then_inc(s["heads1"], 1)
            pool.wait_ge(s["heads1"], 1)
            pool.affine_select(out=blocks, in_=blocks, compare_op=ALU.is_ge, fill=0.0, base=DH - 1,
                               pattern=[[DH, H], [0, DH]], channel_multiplier=-1).then_inc(s["heads_ready"], 1)

            def load_expert(k):
                src = w1[k] if k < E else w2[k - E].rearrange("(f p) d -> p f d", p=128)
                dst, loaded, _ = staged(k)
                if k >= E:
                    dst = dst.rearrange("p (f d) -> p f d", f=FC)
                if k >= GATE_RING:
                    pool.wait_ge(s["set_wl"], k + 1 - GATE_RING)
                pool.dma_start(dst, src).then_inc(loaded, 16)

            for k in range(GATE_RING):
                load_expert(k)

            def inv_std(key, n):
                _, mv, ve, rs = ln[key]
                wait(pool, s[f"{key}_mv"], n + 1)
                pool.tensor_tensor(ve[:], mv[:, :, 1], eps_t[:], ALU.add).then_inc(s[f"{key}_ve"], 1)
                wait(pool, s[f"{key}_ve"], n + 1)
                pool.tensor_tensor(ve[:], ve[:], minus_half[:], ALU.pow).then_inc(s[f"{key}_rs"], 1)

            def per_chunk(v):
                return v[:].unsqueeze(1).to_broadcast([128, TC, D])

            def tick(T, u, t, i, i0):
                if i0 == 0 and T == t and t % SPLIT_EVERY == 0:
                    k = t // SPLIT_EVERY
                    high, low = split_of(k)
                    pool.wait_ge(s["set_wh"], k + 1)
                    pool.tensor_tensor(low, staged(k)[0], high.bitcast(F32), ALU.subtract).then_inc(s["set_wl"], 1)
                if i0 == 0 and T == t and t % SPLIT_EVERY == 1 and t // SPLIT_EVERY + GATE_RING < 2 * E:
                    load_expert(t // SPLIT_EVERY + GATE_RING)
                if T == 22 - TICKS:
                    inv_std("f", u.n)
                    if i0 < 0:
                        pool.wait_ge(s["ld_bc"], 16 * 6)
                        pool.tensor_scalar(g2_b[:], g2_b[:], 0.5, None, ALU.mult).then_inc(s["g2_half"], 1)
                        pool.tensor_scalar(b2_b[:], b2_b[:], 0.5, None, ALU.mult).then_inc(s["g2_half"], 1)
                if T == 100:
                    inv_std("c", u.n)
                m = T - EXPERTS_AT - 1
                if 0 <= m < 64 and m % 2 == 0 and not is_last(T, t, i0):
                    n = m // 2
                    wait(pool, s["h_hi"], u.count(32, n + 1))
                    wait(pool, s["y_mm"], u.count(32, n + 1 - RING))
                    pool.tensor_tensor(hidl[:, n % RING, :], hid[:, n % 2, :], hidh[:, n % RING, :].bitcast(F32),
                                       ALU.subtract).then_inc(s["h_lo"], 1)
                m = T - EXPERTS_AT - DOWN_LAG - 7
                if 0 <= m < 64 and m % 8 == 0:
                    e = m // 8
                    wait(pool, s["y_gated"], u.count(8, e + 1))
                    wait(pool, s["y_acc"], u.count(8, e))
                    ya = yacc[u.parity]
                    pool.tensor_tensor(ya[:], ya[:], gated[:], ALU.add).then_inc(s["y_acc"], 1)
                if T == 185:
                    inv_std("e", u.n)
                if T == 187:
                    wait(pool, s["e_zn"], u.count(1, 1))
                    wait(pool, s["g2_half"], 2)
                    pool.tensor_tensor(zn[:].rearrange("p (c d) -> p c d", c=TC),
                                       zn[:].rearrange("p (c d) -> p c d", c=TC), per_chunk(g2_b), ALU.mult)\
                        .then_inc(s["e_zg"], 1)
                    wait(pool, s["e_zg"], u.count(1, 1))
                    pool.tensor_tensor(zn[:].rearrange("p (c d) -> p c d", c=TC),
                                       zn[:].rearrange("p (c d) -> p c d", c=TC), per_chunk(b2_b), ALU.add)\
                        .then_inc(s["e_zb"], 1)

            def mid(t, b, i, i0):
                if t == 4:
                    inv_std("m", b.n)

            run(pool, lambda i, p, i0: walk(i, p, i0, tick, mid))

        @block.scalar
        def _(act):
            def set_up():
                act.wait_ge(s["set_cT"], 1)
                act.activation(cwh[:].rearrange("p j o -> p (j o)"), turned_conv[:, 0:3 * D], ACT.Copy)\
                    .then_inc(s["set_ch"], 1)
                act.wait_ge(s["set_qT"], 1)
                act.activation(qkh[:].rearrange("p j o -> p (j o)"), turned_qkv[:, 0:2 * D], ACT.Copy)\
                    .then_inc(s["set_qh"], 1)
                act.wait_ge(s["set_cols"], 1)

            def tick(T, u, t, i, i0):
                if i0 == 0 and T == t and t % SPLIT_EVERY == 0:
                    k = t // SPLIT_EVERY
                    src, loaded, value = staged(k)
                    act.wait_ge(loaded, value)
                    act.activation(split_of(k)[0], src, ACT.Copy).then_inc(s["set_wh"], 1)
                if T == 26 - TICKS:
                    wait(act, s["f_xT"], u.count(1, 1))
                    wait(act, s["f_conv"], u.count(1, 0))
                    if in_iteration(i0, "mid"):
                        wait(act, s["m_v"], i - MID_FIRST + 1)
                    wait(act, s["zero_v"], 1)
                    act.activation(xh[:, 1:S + 1], misc[:], ACT.Copy).then_inc(s["f_xh"], 1)
                    if i0 < 0:
                        set_up()
                if T == 36 - TICKS:
                    wait(act, s["f_conv"], u.count(1, 1))
                    wait(act, s["f_qk"], u.count(2, 0))
                    act.activation(ch[:], misc[:], ACT.Identity, bias=col(V_CONV)).then_inc(s["f_ch"], 1)
                    wait(act, s["c_x1"], u.n - 1)
                    act.activation(conv[u.parity][:], misc[:], ACT.Identity, bias=col(V_CONV))\
                        .then_inc(s["f_c"], 1)
                for k, at, bias in ((0, 38 - TICKS, V_BQ), (1, 41 - TICKS, V_BK)):
                    if T == at:
                        wait(act, s["f_qk"], u.count(2, k + 1))
                        wait(act, s["parts_out"], u.count(32, 0))
                        act.activation(parts[k][:, 0, :], misc[:], ACT.Identity, bias=col(bias))\
                            .then_inc(s["f_p1"], 1)
                    if T == at + 1:
                        wait(act, s["f_r1"], u.count(2, k + 1))
                        act.activation(parts[k][:, 1, :], rest[:], ACT.Copy).then_inc(s["f_p2"], 1)
                        if i0 < 0 and k == 1:
                            act.wait_ge(s["ld_mid"], 48)
                            act.activation(mwh[:], mws, ACT.Copy).then_inc(s["set_mh"], 1)
                if T in NM_AT:
                    g = NM_AT[T]
                    wait(act, s["a_nmT"], u.count(4, g + 1))
                    wait(act, s["a_m_in"], u.count(48 * G, 48 * g))
                    act.activation(m_parts[:, 0, :], misc[0:HG * TC, 0:128], ACT.Copy).then_inc(s["a_m1"], 1)
                if T - 1 in NM_AT:
                    g = NM_AT[T - 1]
                    wait(act, s["a_r1"], u.count(4, g + 1))
                    act.activation(m_parts[:, 1, :], m_rest[:], ACT.Copy).then_inc(s["a_m2"], 1)
                if P2_AT <= T < P2_AT + 64:
                    n, j = divmod(T - P2_AT, HG)
                    wait(act, s["a_s2"], u.count(64, T - P2_AT + 1))
                    wait(act, s["a_pv"], u.count(16, n - 1))
                    act.activation(probs[:, n % 2, j, :], score2[(T - P2_AT) % 2][:], ACT.Exp, scale=SCALE)\
                        .then_inc(s["a_exp"], 1)
                if T - 42 in (0, 16, 32, 48):
                    g = (T - 42) // 16
                    wait(act, s["a_pv"], u.count(16, 4 * g + 4))
                    wait(act, s["a_ctxT"], u.count(4, g))
                    wait(act, s["c_x1"], u.n)
                    act.activation(ctxT[:], ctx_ps[:], ACT.Copy).then_inc(s["a_ctx"], 1)
                if T == 95:
                    wait(act, s["c_cT"], u.count(1, 1))
                    act.activation(ctxT[:], misc[:], ACT.Copy).then_inc(s["c_cTs"], 1)
                if T == 110:
                    wait(act, s["c_x1f"], u.count(1, 1))
                    wait(act, s["h_mm"], u.count(32, 0))
                    act.activation(x1h[:], misc[:], ACT.Identity, bias=col(V_B1), scale=col(V_G1))\
                        .then_inc(s["c_x1h"], 1)
                if T == 115:
                    wait(act, s["c_lg2"], u.count(1, 1))
                    act.activation(eg[:], lg2[:], ACT.Exp).then_inc(s["c_eg"], 1)
                if T == 118:
                    wait(act, s["c_prT"], u.count(1, 1))
                    wait(act, s["gate_out"], u.count(16, 0))
                    act.activation(gateT[:], misc[0:E, :], ACT.Copy).then_inc(s["c_prTs"], 1)
                m = T - EXPERTS_AT
                if 0 <= m < 64 and m % 2 == 0:
                    n = m // 2
                    wait(act, s["h_mm"], u.count(32, n + 1))
                    wait_lo(act, u, n - 1, is_last(T, t, i0))
                    act.activation(hid[:, n % 2, :], hid_ps[:], ACT.Relu, bias=col(n)).then_inc(s["h_full"], 1)
                if T == 183:
                    wait(act, s["e_T"], u.count(1, 1))
                    if i0 < UNITS + 1:
                        wait(act, s["c_xnT"], u.n + 2)
                    act.activation(zn[:], misc[:], ACT.Copy).then_inc(s["e_t"], 1)

            def mid(t, b, i, i0):
                if t == 8:
                    wait(act, s["m_xT"], b.count(1, 1))
                    wait(act, s["f_conv"], i + 1)
                    act.activation(mxh, misc[:], ACT.Copy).then_inc(s["m_xh"], 1)
                if t == 11:
                    wait(act, s["m_q"], b.count(1, 1))
                    act.activation(mq[:], misc[:], ACT.Identity, bias=col(V_MBQ)).then_inc(s["m_mq"], 1)
                if t == 21:
                    wait(act, s["m_sc"], b.count(1, 1))
                    act.activation(m_xn[:], m_xn[:], ACT.Exp, scale=SCALE).then_inc(s["m_ex"], 1)

            def iteration(i, p, i0):
                if i0 == 0:
                    act.wait_ge(s["set_oT"], 1)
                    act.wait_ge(s["set_ml"], 1)
                walk(i, p, i0, tick, mid)

            run(act, iteration)

        @block.vector
        def _(dve):
            for p in range(2):
                dve.memset(V[p][:], 1.0)
            for z in (xh, xl):
                dve.memset(z[:].bitcast(F32), 0.0)
            dve.memset(ctx_ps[:], 0.0).then_inc(s["zero_v"], 1)
            dve.memset(Kp[:].bitcast(F32), 0.0).then_inc(s["k_zero"], 1)
            dve.wait_ge(s["k_zero"], 1)
            dve.memset(Kp[MAX_ROW:MAX_ROW + 3].bitcast(F32), TWO_ONES).then_inc(s["pack_zero"], 1)

            def set_up():
                dve.wait_ge(s["set_vT"], 1)
                dve.tensor_copy(cols[:], turned_vec[:, 0:NV]).then_inc(s["set_cols"], 1)
                dve.wait_ge(s["set_ch"], 1)
                dve.tensor_tensor(cwl[:].rearrange("p j o -> p (j o)"), turned_conv[:, 0:3 * D],
                                  cwh[:].bitcast(F32).rearrange("p j o -> p (j o)"), ALU.subtract)\
                    .then_inc(s["set_cl"], 1)
                dve.wait_ge(s["set_qh"], 1)
                dve.tensor_tensor(qkl[:].rearrange("p j o -> p (j o)"), turned_qkv[:, 0:2 * D],
                                  qkh[:].bitcast(F32).rearrange("p j o -> p (j o)"), ALU.subtract)
                dve.tensor_copy(wvT[:], turned_qkv[:, 2 * D:3 * D]).then_inc(s["set_ql"], 1)

            def set_up_rest():
                dve.wait_ge(s["set_oT"], 1)
                dve.tensor_copy(woT[:], turned_wo[:, 0:D])
                dve.wait_ge(s["set_mh"], 1)
                dve.tensor_tensor(mwl[:], mws, mwh[:].bitcast(F32), ALU.subtract).then_inc(s["set_ml"], 1)
                dve.wait_ge(s["heads_ready"], 1)
                dve.tensor_reduce(dil_mask[:], heads8[:].rearrange("p (a r d) -> p r a d", r=DIL, d=DH), AX.XY,
                                  ALU.max).then_inc(s["mask_ready"], 1)
                dve.wait_ge(s["ld_bc"], 16 * 6)

            def moments(key, n, src):
                st, mv, _, _ = ln[key]
                for c in range(TC):
                    last = dve.bn_stats(st[:, c, :], src(c))
                last.then_inc(s[f"{key}_bn"], 1)
                wait(dve, s[f"{key}_bn"], n + 1)
                dve.sem_inc(s["held_dve"], 1)
                for c in range(TC):
                    last = dve.bn_aggr(mv[:, c, :], st[:, c, :])
                last.then_inc(s[f"{key}_mv"], 1)

            def normalise(key, n, dst, src, done):
                _, mv, rs, _ = ln[key]
                wait(dve, s[f"{key}_rs"], n + 1)
                for c in range(TC):
                    last = dve.tensor_scalar(chunk(dst, c), src(c), mv[:, c, 0:1], rs[:, c:c + 1],
                                             ALU.subtract, ALU.mult)
                last.then_inc(s[done], 1)

            def tick(T, u, t, i, i0):
                m = T - EXPERTS_AT - 1
                if 0 <= m < 64 and m % 2 == 0:
                    n = m // 2
                    wait(dve, s["h_full"], u.count(32, n + 1))
                    wait(dve, s["y_mm"], u.count(32, n + 1 - RING))
                    dve.tensor_copy(hidh[:, n % RING, :], hid[:, n % 2, :]).then_inc(s["h_hi"], 1)
                    if is_last(T, t, i0):
                        wait(dve, s["h_hi"], u.count(32, n + 1))
                        dve.tensor_tensor(hidl[:, n % RING, :], hid[:, n % 2, :],
                                          hidh[:, n % RING, :].bitcast(F32), ALU.subtract).then_inc(s["h_lo_last"], 1)
                m = T - EXPERTS_AT - DOWN_LAG - 6
                if 0 <= m < 64 and m % 8 == 0:
                    e = m // 8
                    wait(dve, s["y_mm"], u.count(32, 4 * e + 4))
                    wait(dve, s["gate_in"], u.count(32, 16 * (e // GATE_RING + 1)))
                    wait(dve, s["y_acc"], u.count(8, e))
                    dve.scalar_tensor_tensor(out=gated[:], in0=y_ps[:], scalar=col(V_B2 + e),
                                             in1=gate_b128[:, e % GATE_RING, :], op0=ALU.add, op1=ALU.mult)\
                        .then_inc(s["y_gated"], 1)
                if T == 184:
                    wait(dve, s["e_t"], u.count(1, 1))
                    moments("e", u.n, lambda c: chunk(zn, c))
                if T == 186:
                    normalise("e", u.n, zn, lambda c: chunk(zn, c), "e_zn")
                if T == 190:
                    wait(dve, s["e_zb"], u.count(1, 1))
                    wait(dve, s["e_in"], u.count(16, 16))
                    dve.tensor_tensor(resid[:], resid[:], zn[:], ALU.add).then_inc(s["e_x"], 1)
                if 0 <= T < 64:
                    h, qc = divmod(T, TC)
                    g = h // HG
                    wait(dve, s["a_s1"], u.count(64, T + 1))
                    if T % 16 == 0:
                        wait(dve, s["a_nmT"], u.count(4, g - 1))
                    dve.tensor_reduce(negmax[:, g % 2, T % 16:T % 16 + 1], score1[T % 2][:], AX.X, ALU.max,
                                      negate=True).then_inc(s["a_max"], 1)
                if T in NM_AT:
                    g = NM_AT[T]
                    wait(dve, s["a_m1"], u.count(4, g + 1))
                    dve.tensor_tensor(m_rest[:], misc[0:HG * TC, 0:128], m_parts[:, 0, :], ALU.subtract)\
                        .then_inc(s["a_r1"], 1)
                if T - 1 in NM_AT:
                    g = NM_AT[T - 1]
                    wait(dve, s["a_m2"], u.count(4, g + 1))
                    dve.tensor_tensor(m_parts[:, 2, :], m_rest[:], m_parts[:, 1, :], ALU.subtract)\
                        .then_inc(s["a_m3"], 1)
                if T in CTX_AT:
                    g = CTX_AT[T]
                    turned = misc[:].rearrange("p (c j r) -> p c j r", c=TC, j=HG)
                    wait(dve, s["a_ctxT"], u.count(4, g + 1))
                    wait(dve, s["c_cT"], u.count(1, 0))
                    dve.reciprocal(rden[:], turned[:, :, :, DH]).then_inc(s["a_rden"], 1)
                    wait(dve, s["a_rden"], u.count(4, g + 1))
                    dve.tensor_tensor(ctxs[:, :, g * HG:(g + 1) * HG, :], turned[:, :, :, 0:DH],
                                      rden[:].unsqueeze(3).to_broadcast([128, TC, HG, DH]), ALU.mult)\
                        .then_inc(s["a_norm"], 1)
                if T == 98:
                    wait(dve, s["c_x1"], u.count(1, 1))
                    wait(dve, s["e_x"], u.n - 1)
                    dve.tensor_tensor(x1n[:].rearrange("p (c d) -> p c d", c=TC),
                                      misc[:].rearrange("p (c d) -> p c d", c=TC),
                                      bo_b[:].unsqueeze(1).to_broadcast([128, TC, D]), ALU.add)\
                        .then_inc(s["c_x1p"], 1)
                if T == 99:
                    wait(dve, s["c_x1p"], u.count(1, 1))
                    moments("c", u.n, lambda c: chunk(x1n, c))
                if T == 101:
                    normalise("c", u.n, x1n, lambda c: chunk(x1n, c), "c_xn")
                if T == 110:
                    wait(dve, s["c_xnT"], u.count(1, 1))
                    wait(dve, s["e_T"], u.n - 1)
                    dve.tensor_scalar(yacc[u.parity][:], misc[:], col(V_G1), col(V_B1), ALU.mult, ALU.add)\
                        .then_inc(s["c_x1f"], 1)
                if T == 111:
                    wait(dve, s["c_x1h"], u.count(1, 1))
                    dve.tensor_tensor(x1l[:], yacc[u.parity][:], x1h[:].bitcast(F32), ALU.subtract)\
                        .then_inc(s["c_x1l"], 1)
                if T == 114:
                    wait(dve, s["c_gate"], u.count(1, 1))
                    dve.tensor_tensor(lg[:], misc[:, 0:TC * E].rearrange("p (c e) -> p c e", c=TC),
                                      gb_b[:].unsqueeze(1).to_broadcast([128, TC, E]), ALU.add)\
                        .then_inc(s["c_lg"], 1)
                    wait(dve, s["c_lg"], u.count(1, 1))
                    dve.tensor_reduce(gmax[:], lg[:], AX.X, ALU.max).then_inc(s["c_gmax"], 1)
                    wait(dve, s["c_gmax"], u.count(1, 1))
                    dve.tensor_tensor(lg2[:], lg[:], gmax[:].unsqueeze(2).to_broadcast([128, TC, E]),
                                      ALU.subtract).then_inc(s["c_lg2"], 1)
                if T == 116:
                    wait(dve, s["c_eg"], u.count(1, 1))
                    dve.tensor_reduce(gsum[:], eg[:], AX.X, ALU.add).then_inc(s["c_gsum"], 1)
                    wait(dve, s["c_gsum"], u.count(1, 1))
                    dve.reciprocal(ginv[:], gsum[:]).then_inc(s["c_ginv"], 1)
                    wait(dve, s["c_ginv"], u.count(1, 1))
                    dve.tensor_tensor(gate[u.parity][:], eg[:], ginv[:].unsqueeze(2).to_broadcast([128, TC, E]),
                                      ALU.mult).then_inc(s["c_pr"], 1)
                if T == 21 - TICKS:
                    wait(dve, s["f_in"], u.count(16, 16))
                    moments("f", u.n, lambda c: chunk(f_xn, c))
                if T == 23 - TICKS:
                    normalise("f", u.n, f_xn, lambda c: chunk(f_xn, c), "f_xn")
                if T == 26 - TICKS:
                    wait(dve, s["f_xh"], u.count(1, 1))
                    dve.tensor_tensor(xl[:, 1:S + 1], misc[:], xh[:, 1:S + 1].bitcast(F32), ALU.subtract)\
                        .then_inc(s["f_xl"], 1)
                    if i0 < 0:
                        set_up()
                if T == 36 - TICKS:
                    wait(dve, s["f_c"], u.count(1, 1))
                    dve.scalar_tensor_tensor(out=cl[:], in0=misc[:], scalar=col(V_CONV),
                                             in1=ch[:].bitcast(F32), op0=ALU.add, op1=ALU.subtract)\
                        .then_inc(s["f_cl"], 1)
                for k, at, bias in ((0, 38 - TICKS, V_BQ), (1, 41 - TICKS, V_BK)):
                    if T == at:
                        wait(dve, s["f_p1"], u.count(2, k + 1))
                        wait(dve, s["f_p3"], u.count(2, k))
                        dve.scalar_tensor_tensor(out=rest[:], in0=misc[:], scalar=col(bias),
                                                 in1=parts[k][:, 0, :], op0=ALU.add, op1=ALU.subtract)\
                            .then_inc(s["f_r1"], 1)
                    if T == at + 1:
                        wait(dve, s["f_p2"], u.count(2, k + 1))
                        dve.tensor_tensor(parts[k][:, 2, :], rest[:], parts[k][:, 1, :], ALU.subtract)\
                            .then_inc(s["f_p3"], 1)
                        if i0 < 0 and k == 1:
                            set_up_rest()
                if T == 58 - TICKS:
                    wait(dve, s["f_v"], u.count(1, 1))
                    wait(dve, s["a_pv"], (u.n - 1) * 16)
                    dve.tensor_tensor(V[u.parity][:, :, :, 0:DH],
                                      misc[:].rearrange("p (c h d) -> p c h d", c=TC, h=H),
                                      bv_b[:].rearrange("p (h d) -> p h d", h=H).unsqueeze(1)
                                      .to_broadcast([128, TC, H, DH]), ALU.add).then_inc(s["f_vs"], 1)

            def by_offset(ap):
                return ap.rearrange("p (n s r) -> p n r s", n=NSG, r=DIL)

            def over_steps(v):
                return v[:].unsqueeze(3).to_broadcast([128, NSG, DIL, SEG // DIL])

            def mid(t, b, i, i0):
                if t == 3:
                    wait(dve, s["m_in"], b.count(16, 16))
                    moments("m", b.n, lambda c: chunk(m_xn, c))
                if t == 5:
                    normalise("m", b.n, m_xn, lambda c: chunk(m_xn, c), "m_xn")
                if t == 9:
                    wait(dve, s["m_xh"], b.count(1, 1))
                    dve.tensor_tensor(mxl, misc[:], mxh.bitcast(F32), ALU.subtract).then_inc(s["m_xl"], 1)
                if t == 14:
                    wait(dve, s["m_k"], b.count(1, 1))
                    wait(dve, s["m_mq"], b.count(1, 1))
                    dve.scalar_tensor_tensor(out=mq[:], in0=misc[:], scalar=col(V_MBK), in1=mq[:],
                                             op0=ALU.add, op1=ALU.mult).then_inc(s["m_qk"], 1)
                if t == 20:
                    wait(dve, s["m_s"], b.count(1, 1))
                    dve.tensor_reduce(mmax[:], by_offset(misc[:]), AX.X, ALU.max).then_inc(s["m_max"], 1)
                    wait(dve, s["m_max"], b.count(1, 1))
                    dve.tensor_tensor(by_offset(m_xn[:]), by_offset(misc[:]), over_steps(mmax), ALU.subtract)\
                        .then_inc(s["m_sc"], 1)
                if t == 22:
                    wait(dve, s["m_ex"], b.count(1, 1))
                    dve.tensor_reduce(msum[:], by_offset(m_xn[:]), AX.X, ALU.add).then_inc(s["m_sum"], 1)
                    wait(dve, s["m_sum"], b.count(1, 1))
                    dve.reciprocal(minv[:], msum[:]).then_inc(s["m_inv"], 1)
                    wait(dve, s["m_inv"], b.count(1, 1))
                    wait(dve, s["mask_ready"], 1)
                    dve.tensor_tensor(mwt[:], minv[:], dil_mask[:].unsqueeze(1).to_broadcast([128, NSG, DIL]),
                                      ALU.mult).then_inc(s["m_wt"], 1)
                if t == 23:
                    wait(dve, s["m_wt"], b.count(1, 1))
                    dve.tensor_tensor(by_offset(m_xn[:]), by_offset(m_xn[:]), over_steps(mwt), ALU.mult)\
                        .then_inc(s["m_w"], 1)
                if t == 24:
                    wait(dve, s["m_v"], b.count(1, 1))
                    wait(dve, s["m_w"], b.count(1, 1))
                    dve.scalar_tensor_tensor(out=m_xn[:], in0=misc[:], scalar=col(V_MBV), in1=m_xn[:],
                                             op0=ALU.add, op1=ALU.mult).then_inc(s["m_o"], 1)
                if t == 29:
                    wait(dve, s["m_out"], b.count(1, 1))
                    dve.tensor_tensor(mq[:].rearrange("p (c d) -> p c d", c=TC),
                                      misc[:].rearrange("p (c d) -> p c d", c=TC),
                                      mbo_b[:].unsqueeze(1).to_broadcast([128, TC, D]), ALU.add)\
                        .then_inc(s["m_t"], 1)
                if t == 31:
                    wait(dve, s["m_t"], b.count(1, 1))
                    wait(dve, s["m_in2"], b.count(16, 16))
                    dve.tensor_tensor(resid[:], resid[:], mq[:], ALU.add).then_inc(s["m_x"], 1)

            run(dve, lambda i, p, i0: walk(i, p, i0, tick, mid))

        @block.tensor
        def _(pe):
            def three(dst, hi, lo, rhi, rlo, start=True, stop=True, before_rlo=None):
                pe.matmul(dst, hi, rhi, start=start, stop=False)
                pe.matmul(dst, lo, rhi, start=False, stop=False)
                if before_rlo:
                    wait(pe, *before_rlo)
                return pe.matmul(dst, hi, rlo, start=False, stop=stop)

            def set_up():
                pe.wait_ge(s["ld_vec"], 16 * (E + 8))
                pe.transpose(turned_vec[:, 0:NV], vec_rows, ident[0:NV, 0:NV]).then_inc(s["set_vT"], 1)
                pe.wait_ge(s["ld_conv"], 16)
                for j in range(3):
                    last = pe.transpose(turned_conv[:, j * D:(j + 1) * D], conv_raw[:, :, j], ident[:])
                last.then_inc(s["set_cT"], 1)
                pe.wait_ge(s["ld_qkv"], 16)
                for j in range(3):
                    last = pe.transpose(turned_qkv[:, j * D:(j + 1) * D], wqkv_raw[:, j, :], ident[:])
                last.then_inc(s["set_qT"], 1)
                pe.wait_ge(s["ld_wo"], 16)
                pe.transpose(turned_wo[:, 0:D], wo_raw, ident[:]).then_inc(s["set_oT"], 1)
                pe.wait_ge(s["ld_small"], 32)
                pe.wait_ge(s["set_ql"], 1)

            pe.wait_ge(s["ident_ready"], 1)

            def tick(T, u, t, i, i0):
                p = u.parity
                if T == 26 - TICKS:
                    wait_misc(pe, t, i, i0)
                    wait(pe, s["f_xn"], u.count(1, 1))
                    for c in range(TC):
                        last = pe.transpose(chunk(misc, c), chunk(f_xn, c), ident[:])
                    last.then_inc(s["f_xT"], 1)
                    if i0 < 0:
                        set_up()
                if T == 36 - TICKS:
                    wait_misc(pe, t, i, i0)
                    wait(pe, s["f_xl"], u.count(1, 1))
                    for j in range(3):
                        last = three(misc[:], cwh[:, j, :], cwl[:, j, :], xh[:, j:j + S], xl[:, j:j + S],
                                     start=(j == 0), stop=(j == 2))
                    last.then_inc(s["f_conv"], 1)
                for k, at in ((0, 38 - TICKS), (1, 41 - TICKS)):
                    if T == at:
                        wait_misc(pe, t, i, i0)
                        wait(pe, s["f_cl"], u.count(1, 1))
                        three(misc[:], qkh[:, k, :], qkl[:, k, :], ch[:], cl[:]).then_inc(s["f_qk"], 1)
                if T == 58 - TICKS:
                    wait_misc(pe, t, i, i0)
                    wait(pe, s["f_c"], u.count(1, 1))
                    for c in range(TC):
                        last = pe.matmul(chunk(misc, c), chunk(conv[p], c), wvT[:], start=True, stop=True)
                    last.then_inc(s["f_v"], 1)
                if T in NM_AT:
                    g = NM_AT[T]
                    wait_misc(pe, t, i, i0)
                    wait(pe, s["a_max"], u.count(64, 16 * g + 16))
                    pe.transpose(misc[0:HG * TC, 0:128], negmax[:, g % 2, :], ident[:]).then_inc(s["a_nmT"], 1)
                if T in CTX_AT:
                    g = CTX_AT[T]
                    wait_misc(pe, t, i, i0)
                    wait(pe, s["a_ctx"], u.count(4, g + 1))
                    for c in range(TC):
                        last = pe.transpose(chunk(misc, c), chunk(ctxT, c), ident[:])
                    last.then_inc(s["a_ctxT"], 1)
                if T == 95:
                    wait_misc(pe, t, i, i0)
                    wait(pe, s["a_norm"], u.count(4, 4))
                    for c in range(TC):
                        last = pe.transpose(chunk(misc, c), ctxs[:, c, :, :].rearrange("p h d -> p (h d)"), ident[:])
                    last.then_inc(s["c_cT"], 1)
                if T == 98:
                    wait_misc(pe, t, i, i0)
                    wait(pe, s["c_cTs"], u.count(1, 1))
                    for c in range(TC):
                        pe.matmul(chunk(misc, c), chunk(ctxT, c), woT[:], start=True, stop=False)
                        last = pe.matmul(chunk(misc, c), chunk(conv[p], c), ident[:], start=False, stop=True)
                    last.then_inc(s["c_x1"], 1)
                if T == 110:
                    wait_misc(pe, t, i, i0)
                    wait(pe, s["c_xn"], u.count(1, 1))
                    for c in range(TC):
                        last = pe.transpose(chunk(misc, c), chunk(x1n, c), ident[:])
                    last.then_inc(s["c_xnT"], 1)
                if T == 114:
                    wait_misc(pe, t, i, i0)
                    for c in range(TC):
                        last = pe.matmul(misc[:, c * E:(c + 1) * E], chunk(yacc[p], c), gws[:], start=True, stop=True)
                    last.then_inc(s["c_gate"], 1)
                if T == 118:
                    wait_misc(pe, t, i, i0)
                    wait(pe, s["c_pr"], u.count(1, 1))
                    for c in range(TC):
                        last = pe.transpose(misc[0:E, c * 128:(c + 1) * 128], gate[p][:, c, :], ident[:])
                    last.then_inc(s["c_prT"], 1)
                if T == 183:
                    wait_misc(pe, t, i, i0)
                    wait(pe, s["y_acc"], u.count(8, 8))
                    for c in range(TC):
                        last = pe.transpose(chunk(misc, c), chunk(yacc[p], c), ident[:])
                    last.then_inc(s["e_T"], 1)
                if P2_AT <= T < P2_AT + 64:
                    k = T - P2_AT
                    n, j = divmod(k, HG)
                    g, kc = divmod(n, TC)
                    if k % 16 == 0:
                        wait(pe, s["a_m_in"], u.count(48 * G, 48 * (g + 1)))
                    wait(pe, s["a_exp"], u.count(64, k - 1))
                    pe.matmul(score2[k % 2][:], Kp[:, g * HG + j, kc * 128:(kc + 1) * 128],
                              Qp[:, g * HG + j, :], start=True, stop=True).then_inc(s["a_s2"], 1)
                if 0 <= T < 64:
                    h, qc = divmod(T, TC)
                    if T % 16 == 0:
                        wait(pe, s["pack_in"], u.count(192 * G, 192 * (h // HG + 1)))
                    wait(pe, s["a_max"], u.count(64, T - 1))
                    pe.matmul(score1[T % 2][:], Qp[0:SCORE_ROWS, h, qc * 128:(qc + 1) * 128],
                              Kp[0:SCORE_ROWS, h, :], start=True, stop=True).then_inc(s["a_s1"], 1)
                k = T - P2_AT - PV_LAG
                if 0 <= k < 64 and k % HG == 0:
                    n = k // HG
                    g, kc = divmod(n, TC)
                    wait(pe, s["a_exp"], u.count(64, 4 * n + 4))
                    if n == 0:
                        wait(pe, s["f_vs"], u.count(1, 1))
                        wait(pe, s["zero_v"], 1)
                    if kc == 0:
                        wait(pe, s["a_ctx"], u.count(4, g))
                    for j in range(HG):
                        last = pe.matmul(ctx_ps[32 * j:32 * j + DH + 1, :], V[p][:, kc, g * HG + j, :],
                                         probs[:, n % 2, j, :], start=(kc == 0), stop=(kc == TC - 1))
                    last.then_inc(s["a_pv"], 1)
                m = T - EXPERTS_AT
                if 0 <= m < 64 and m % 2 == 0:
                    n = m // 2
                    if n == 0:
                        wait(pe, s["c_x1h"], u.count(1, 1))
                    if i0 < 2:
                        wait(pe, s["set_wl"], E)
                    wait(pe, s["h_full"], u.count(32, n))
                    w = slice(n * 128, (n + 1) * 128)
                    three(hid_ps[:], w1h[:, w], w1l[:, w], x1h[:], x1l[:],
                          before_rlo=(s["c_x1l"], u.count(1, 1)) if n == 0 else None).then_inc(s["h_mm"], 1)
                m = T - EXPERTS_AT - DOWN_LAG
                if 0 <= m < 64 and m % 2 == 0:
                    n = m // 2
                    e, f = divmod(n, FC)
                    wait_lo(pe, u, n + 1, is_last(T, t, i0))
                    if f == 0:
                        wait(pe, s["y_gated"], u.count(8, e))
                        if i0 < 2:
                            wait(pe, s["set_wl"], 2 * E)
                    three(y_ps[:], w2h[:, n, :], w2l[:, n, :], hidh[:, n % RING, :], hidl[:, n % RING, :],
                          start=(f == 0), stop=(f == FC - 1)).then_inc(s["y_mm"], 1)

            def mid(t, b, i, i0):
                if t == 8:
                    wait_misc(pe, t, i, i0)
                    wait(pe, s["m_xn"], b.count(1, 1))
                    for c in range(TC):
                        last = pe.transpose(chunk(misc, c), chunk(m_xn, c), ident[:])
                    last.then_inc(s["m_xT"], 1)
                for k, at, done in ((0, 11, "m_q"), (1, 14, "m_k"), (2, 24, "m_v")):
                    if t == at:
                        wait_misc(pe, t, i, i0)
                        wait(pe, s["m_xl"], b.count(1, 1))
                        three(misc[:], mwh[:, k, :], mwl[:, k, :], mxh, mxl).then_inc(s[done], 1)
                if t == 20:
                    wait_misc(pe, t, i, i0)
                    wait(pe, s["m_qk"], b.count(1, 1))
                    pe.matmul(misc[:], heads8[:], mq[:], start=True, stop=True).then_inc(s["m_s"], 1)
                if t == 29:
                    wait_misc(pe, t, i, i0)
                    wait(pe, s["m_o"], b.count(1, 1))
                    for c in range(TC):
                        last = pe.matmul(chunk(misc, c), chunk(m_xn, c), mwo[:], start=True, stop=True)
                    last.then_inc(s["m_out"], 1)

            run(pe, lambda i, p, i0: walk(i, p, i0, tick, mid))


_INS = ["L0_attn_x", "L0_attn_Wq", "L0_attn_bq", "L0_attn_Wk", "L0_attn_bk", "L0_attn_Wv", "L0_attn_bv",
        "L0_attn_Wo", "L0_attn_bo", "L0_ffn_conv_w", "L0_ffn_conv_b", "L0_ffn_wqkv", "L0_ffn_bqkv", "L0_ffn_wo",
        "L0_ffn_bo", "L0_ffn_ln1_g", "L0_ffn_ln1_b", "L0_ffn_gate_w", "L0_ffn_gate_b", "L0_ffn_w1", "L0_ffn_b1",
        "L0_ffn_w2", "L0_ffn_b2", "L0_ffn_ln2_g", "L0_ffn_ln2_b"]


def kernel(**inputs):
    import concourse.bacc as bacc
    from concourse.bass_utils import run_bass_kernel_spmd

    nc = bacc.Bacc("TRN2", target_bir_lowering=False, num_devices=1)
    arrays, args = {}, []
    for name in _INS:
        a = np.ascontiguousarray(inputs[name])
        arrays[f"in_{name}"] = a
        args.append(nc.dram_tensor(f"in_{name}", a.shape, mybir.dt.from_np(a.dtype), kind="ExternalInput").ap())
    args.append(nc.dram_tensor("out", (B, S, D), F32, kind="ExternalOutput").ap())
    macaron(nc, *args)
    return run_bass_kernel_spmd(nc, [arrays], core_ids=[0]).results[0]["out"]
```

```python
from contextlib import ExitStack

import numpy as np

import concourse.bass as bass
from concourse import mybir

ALU = mybir.AluOpType
ACT = mybir.ActivationFunctionType
AX = mybir.AxisListType
F32 = mybir.dt.float32
F32R = mybir.dt.float32r
BF16 = mybir.dt.bfloat16

B, S, D = 8, 512, 128
H, DH = 16, 8
E, FF = 8, 512
TC = S // 128
FC = FF // 128
G, HG = 4, 4
SEG, DIL = 64, 4
EPS = 1e-5
SCALE = float(DH) ** -0.5
UNITS = 2 * B

RUNS_OF_PARTS = (((0, 3, 0, 0), (3, 2, 1, 0), (5, 1, 2, 1)), ((0, 3, 0, 1), (3, 2, 0, 1), (5, 1, 0, 1)))
PACK_LOADS = 16 * 2 * 3
SCORE_ROWS = 96
MAX_ROW = 96
TWO_ONES = float(np.array([0x3F803F80], np.uint32).view(np.float32)[0])

TICKS = 64
P2_AT = 24
PV_LAG = 5
EXPERTS_AT = 112
DOWN_LAG = 6
RING = 4
GATE_RING = 4
MID_FIRST = 6


class Unit:

    def __init__(self, number, parity):
        self.n, self.parity = number, parity

    def count(self, per_unit, k):
        return per_unit * self.n + k


def wait(eng, sem, value):
    if isinstance(value, int) and value <= 0:
        return
    eng.wait_ge(sem, value)


def macaron(nc, x, Wq, bq, Wk, bk, Wv, bv, Wo, bo, conv_w, conv_b, wqkv, bqkv, wo, bo2, ln1_g, ln1_b,
            gate_w, gate_b, w1, b1, w2, b2, ln2_g, ln2_b, out):
    with ExitStack() as ctx:
        def sb(name, shape, dt=F32):
            return ctx.enter_context(nc.sbuf_tensor(name, shape, dt))

        def psum(name):
            return ctx.enter_context(nc.psum_tensor(name, [128, 512], F32))

        def sem(name):
            return ctx.enter_context(nc.semaphore(name))

        score1 = [psum("score1a"), psum("score1b")]
        score2 = [psum("score2a"), psum("score2b")]
        ctx_ps = psum("ctx_ps")
        hid_ps = psum("hid_ps")
        y_ps = psum("y_ps")
        misc = psum("misc")

        w1h, w1l = sb("w1h", [128, E * FF], F32R), sb("w1l", [128, E * FF], F32R)
        w2h, w2l = sb("w2h", [128, E * FC, D], F32R), sb("w2l", [128, E * FC, D], F32R)
        gws = sb("gws", [128, E])
        cwh, cwl = sb("cwh", [128, 3, D], F32R), sb("cwl", [128, 3, D], F32R)
        qkh, qkl = sb("qkh", [128, 2, D], F32R), sb("qkl", [128, 2, D], F32R)
        wvT, woT = sb("wvT", [128, D]), sb("woT", [128, D])
        mwh, mwl = sb("mwh", [128, 3, D], F32R), sb("mwl", [128, 3, D], F32R)
        mwo = sb("mwo", [128, D])
        NV = E * FC + 8 + E
        cols = sb("cols", [128, NV])
        (V_CONV, V_BQ, V_BK, V_G1, V_B1, V_MBQ, V_MBK, V_MBV) = range(E * FC, E * FC + 8)
        V_B2 = E * FC + 8
        bv_b, bo_b, g2_b, b2_b, mbo_b = (sb(n, [128, D]) for n in ("bv_b", "bo_b", "g2_b", "b2_b", "mbo_b"))
        gb_b = sb("gb_b", [128, E])
        ident, heads8 = sb("ident", [128, 128]), sb("heads8", [128, 128])
        dil_mask = sb("dil_mask", [128, DIL])
        minus_half, eps_t = sb("minus_half", [128, TC]), sb("eps_t", [128, TC])
        resid = sb("resid", [128, S])
        f_xn = sb("f_xn", [128, S])
        xh, xl = sb("xh", [128, S + 2], F32R), sb("xl", [128, S + 2], F32R)
        ch, cl = sb("ch", [128, S], F32R), sb("cl", [128, S], F32R)
        conv = [sb(f"conv{p}", [128, S]) for p in range(2)]
        parts = [sb("q_parts", [128, 3, S], BF16), sb("k_parts", [128, 3, S], BF16)]
        rest = sb("rest", [128, S])
        Qp, Kp = sb("Qp", [128, H, S], BF16), sb("Kp", [128, H, S], BF16)
        V = [sb(f"V{p}", [128, TC, H, DH + 1]) for p in range(2)]
        negmax = sb("negmax", [128, 2, HG * TC])
        m_parts, m_rest = sb("m_parts", [HG * TC, 3, 128], BF16), sb("m_rest", [HG * TC, 128])
        probs = sb("probs", [128, 2, HG, S])
        ctxT = sb("ctxT", [128, S])
        rden = sb("rden", [128, TC, HG])
        ctxs = sb("ctxs", [128, TC, H, DH])
        x1n = sb("x1n", [128, S])
        x1h, x1l = sb("x1h", [128, S], F32R), sb("x1l", [128, S], F32R)
        lg, lg2, eg = sb("lg", [128, TC, E]), sb("lg2", [128, TC, E]), sb("eg", [128, TC, E])
        gmax, gsum, ginv = sb("gmax", [128, TC]), sb("gsum", [128, TC]), sb("ginv", [128, TC])
        gate = [sb(f"gate{p}", [128, TC, E]) for p in range(2)]
        gateT = sb("gateT", [E, S])
        hid = sb("hid", [128, 2, S])
        hidh, hidl = sb("hidh", [128, RING, S], F32R), sb("hidl", [128, RING, S], F32R)
        gate_b128 = sb("gate_b128", [128, GATE_RING, S])
        gated = sb("gated", [128, S])
        yacc = [sb(f"yacc{p}", [128, S]) for p in range(2)]
        zn = x1n
        m_xn = sb("m_xn", [128, S])
        mxh, mxl = xh[:, 1:S + 1], xl[:, 1:S + 1]
        mq = rest
        NSG = S // SEG
        mmax, msum, minv, mwt = (sb(n, [128, NSG, DIL]) for n in ("mmax", "msum", "minv", "mwt"))
        ln = {k: (sb(f"{k}_st", [128, TC, 6]), sb(f"{k}_mv", [128, TC, 2]), sb(f"{k}_ve", [128, TC]),
                  sb(f"{k}_rs", [128, TC])) for k in ("f", "c", "e", "m")}
        turned_vec, turned_conv, turned_qkv, turned_wo = score1[0], score1[1], score2[0], score2[1]
        stage = probs[:].rearrange("p a j q -> p (a j q)")
        conv_raw = stage[:, 0:3 * D].rearrange("p (i j) -> p i j", j=3)
        wqkv_raw = stage[:, 3 * D:6 * D].rearrange("p (j i) -> p j i", j=3)
        mws = stage[:, 6 * D:9 * D].rearrange("p (j i) -> p j i", j=3)
        wo_raw = stage[:, 9 * D:10 * D]
        vec_rows = stage[0:NV, 10 * D:11 * D]
        dram = [nc.dram_tensor(f"{n}_dram", [3, DH, H, S], BF16).ap() for n in ("q_parts", "k_parts")]
        stream = nc.dram_tensor("stream_dram", [B, S, D], F32).ap()
        gate_dram = nc.dram_tensor("gate_dram", [E, S], F32).ap()

        s = {}
        for n in """
            ld_x ld_vec ld_small ld_conv ld_qkv ld_wo ld_mid ld_bc
            zero_v k_zero pack_zero ident0 ident_ready held_dve held_sp consts pads_zero
            heads0 heads1 heads_ready mask_ready g2_half
            set_vT set_cols set_cT set_ch set_cl set_qT set_qh set_ql set_oT set_mh set_ml
            set_wh set_wl
            f_bn f_mv f_ve f_rs c_bn c_mv c_ve c_rs e_bn e_mv e_ve e_rs m_bn m_mv m_ve m_rs
            f_xn f_xT f_xh f_xl f_conv f_c f_ch f_cl f_qk f_p1 f_r1 f_p2 f_p3 f_v f_vs pack_in
            a_s1 a_max a_nmT a_m1 a_r1 a_m2 a_m3 a_m_in a_s2 a_exp a_pv a_ctx a_ctxT a_rden a_norm
            c_cT c_cTs c_x1 c_x1p c_xn c_xnT c_x1h c_x1f c_x1l gate_out
            c_gate f_in e_in e_stored m_in m_in2 m_stored c_lg c_gmax c_lg2 c_eg c_gsum c_ginv c_pr c_prT c_prTs
            h_mm h_hi h_full h_lo h_lo_alone y_mm y_gated y_acc
            e_T e_t e_zn e_zg e_zb e_x
            m_xn m_xT m_xh m_xl m_q m_mq m_k m_qk m_s m_max m_sc m_ex m_sum m_inv m_wt m_w m_v m_o m_out m_t
            m_x
        """.split():
            assert n not in s, n
            s[n] = sem(n)

        def col(k):
            return cols[:, k:k + 1]

        def chunk(ap, c):
            return ap[:, c * 128:(c + 1) * 128]

        def rows_of(dram, b):
            at = dram[b:b + 1] if isinstance(b, int) else dram[bass.ds(b, 1)]
            return at.rearrange("a (c p) d -> p (a c) d", p=128)

        def chunks(tile):
            return tile[:].rearrange("p (c d) -> p c d", c=TC)

        s["parts_out"] = [sem("q_parts_out"), sem("k_parts_out")]
        s["gate_in"] = [sem(f"gate_in{k}") for k in range(GATE_RING)]
        s["ld_w"] = [sem(f"ld_w{k}") for k in range(GATE_RING)]

        LAST_UNIT = UNITS - 1
        misc_uses = sorted(
            [(17 + 16 * g - TICKS * b, b, "a_m3r", 4, g + 1) for g, b in ((0, 0), (1, 0), (2, 0), (3, 1))]
            + [(44 + 16 * g - TICKS * b, b, "a_norm", 4, g + 1) for g, b in ((0, 0), (1, 0), (2, 1), (3, 1))]
            + [(30, 1, "c_cTs", 1, 1), (34, 1, "c_x1p", 1, 1), (46, 1, "c_x1h", 1, 1), (50, 1, "c_lg", 1, 1),
               (54, 1, "c_prTs", 1, 1), (55, 2, "e_t", 1, 1)]
            + [(26, -1, "f_xl", 1, 1), (36, -1, "f_cl", 1, 1), (38, -1, "f_r1", 2, 1), (41, -1, "f_r1", 2, 2),
               (57, -1, "f_vs", 1, 1)]
            + [(8, "mid", "m_xl", 1, 1), (11, "mid", "m_mq", 1, 1), (14, "mid", "m_qk", 1, 1),
               (20, "mid", "m_sc", 1, 1), (24, "mid", "m_o", 1, 1), (31, "mid", "m_t", 1, 1)],
            key=lambda use: use[0])
        assert len({use[0] for use in misc_uses}) == len(misc_uses)

        def in_iteration(i0, back):
            if back == "mid":
                return MID_FIRST <= i0 < MID_FIRST + B
            return 0 <= i0 - back <= LAST_UNIT

        def wait_misc(pe, tick, i, i0):
            before = [(t, b, n, per, k, 0) for t, b, n, per, k in misc_uses if t < tick]
            earlier = [(t, b, n, per, k, 1) for t, b, n, per, k in misc_uses]
            for t, b, n, per, k, ago in reversed(earlier + before):
                if in_iteration(i0 - ago, b):
                    u = i - ago - (MID_FIRST if b == "mid" else b)
                    name = "a_r1" if n == "a_m3r" else n
                    wait(pe, s[name], per * u + k)
                    return

        def run(eng, iteration):
            for i in (-1, 0, 1):
                iteration(i, i % 2, i)
            for a, b in ((2, MID_FIRST), (MID_FIRST, MID_FIRST + B)):
                with eng.Fori(a, b, 2) as r:
                    iteration(r, 0, a + 2)
                    iteration(r + 1, 1, a + 3)
            for i in (14, 15, 16, 17):
                iteration(i, i % 2, i)

        def walk(i, parity, i0, unit_tick, mid_tick=None, first=None):
            for t in range(TICKS):
                if first and in_iteration(i0, 1):
                    first(t + TICKS, Unit(i - 1, (parity - 1) % 2), t, i, i0)
                if mid_tick and in_iteration(i0, "mid"):
                    mid_tick(t, Unit(i - MID_FIRST, parity), i, i0)
                for back in (2, 1, 0, -1):
                    if in_iteration(i0, back):
                        unit_tick(t + TICKS * back, Unit(i - back, (parity - back) % 2), t, i, i0)

        def staged(k):
            return gate_b128[:, k % GATE_RING, :], s["ld_w"][k % GATE_RING], 16 * (k // GATE_RING + 1)

        def split_of(k):
            if k < E:
                return [w[:, k * FF:(k + 1) * FF] for w in (w1h, w1l)]
            return [w[:, (k - E) * FC:(k - E + 1) * FC, :].rearrange("p f d -> p (f d)") for w in (w2h, w2l)]

        FIRST_ALONE = (LAST_UNIT - 1) * E * FC + (2 * TICKS - EXPERTS_AT) // 2

        def alone(u, n):
            return isinstance(u.n, int) and u.n * E * FC + n >= FIRST_ALONE

        def hid_bank(u, n):
            return score1[0] if alone(u, n) and n % 2 else hid_ps

        def wait_lo(eng, u, k):
            if alone(u, k - 1):
                wait(eng, s["h_lo_alone"], u.n * E * FC + k - FIRST_ALONE)
            else:
                wait(eng, s["h_lo"], u.count(32, k))

        def end_block(eng, u):
            wait(eng, s["e_zn"], u.count(1, 1))
            wait(eng, s["g2_half"], 2)
            eng.tensor_tensor(chunks(zn), chunks(zn), g2_b[:].unsqueeze(1).to_broadcast([128, TC, D]), ALU.mult)\
                .then_inc(s["e_zg"], 1)
            wait(eng, s["e_zg"], u.count(1, 1))
            wait(eng, s["e_zb"], u.count(1, 1))
            eng.tensor_tensor(resid[:], resid[:], zn[:], ALU.add).then_inc(s["e_x"], 1)

        SPLIT_EVERY = TICKS // (2 * E)

        NM_AT = {17 + 16 * g: g for g in range(G)}
        CTX_AT = {44 + 16 * g: g for g in range(G)}
        LOADS_AT = ({-19: 0, -6: 1, 9: 2, 25: 3}, {-16: 0, -6: 1, 9: 2, 25: 3})

        block = ctx.enter_context(nc.Block())

        @block.sync
        def _(sp):
            def load(dst, src, name):
                sp.dma_start(dst, src).then_inc(s[name], 16)

            def row(v):
                return v.rearrange("(a n) -> a n", a=1)

            sp.dma_start(chunks(f_xn), rows_of(x, 0)).then_inc(s["f_in"], 16)
            load(conv_raw, conv_w, "ld_conv")
            load(wqkv_raw, wqkv.rearrange("(j o) i -> o j i", j=3), "ld_qkv")
            load(vec_rows[0:E * FC, :], b1.rearrange("e (f p) -> (e f) p", p=128), "ld_vec")
            load(vec_rows[V_CONV:V_CONV + 1, :], row(conv_b), "ld_vec")
            load(vec_rows[V_BQ:V_BQ + 2, :], bqkv[0:2 * D].rearrange("(a n) -> a n", a=2), "ld_vec")
            for k, v in ((V_G1, ln1_g), (V_B1, ln1_b), (V_MBQ, bq), (V_MBK, bk), (V_MBV, bv)):
                load(vec_rows[k:k + 1, :], row(v), "ld_vec")
            load(vec_rows[V_B2:V_B2 + E, :], b2, "ld_vec")
            load(wo_raw, wo, "ld_wo")
            for k, v in enumerate((Wq, Wk, Wv)):
                load(mws[:, k, :], v, "ld_mid")
            for dst, v in ((bv_b, bqkv[2 * D:3 * D]), (bo_b, bo2), (g2_b, ln2_g),
                           (b2_b, ln2_b), (mbo_b, bo)):
                load(dst[:], v.partition_broadcast(128), "ld_bc")
            load(gb_b[:], gate_b.partition_broadcast(128), "ld_bc")
            load(mwo[:], Wo, "ld_small")
            load(gws[:], gate_w, "ld_small")
            load(stream[B // 2:], x[B // 2:], "ld_x")

            def wait_sp(sem, value):
                wait(sp, sem, value)
                sp.sem_inc(s["held_sp"], 1)

            def tick(T, u, t, i, i0):
                for k, at in ((0, 40 - TICKS), (1, 43 - TICKS)):
                    if T == at:
                        wait_sp(s["pack_in"], u.count(PACK_LOADS * G, 0))
                        for part, written in enumerate(("f_p1", "f_p2", "f_p3")):
                            wait_sp(s[written], u.count(2, k + 1))
                            sp.dma_start(dram[k][part].rearrange("d h q -> h d q"), parts[k][:, part, :])\
                                .then_inc(s["parts_out"][k], 16)
                for k, (Tk, g) in [(k, at) for k in range(2) for at in LOADS_AT[k].items()]:
                    if T != Tk:
                        continue
                    wait_sp(s["parts_out"][k], u.count(48, 48))
                    wait_sp(s["a_s2"], (u.n - 1) * 64 + 16 * g + 16)
                    wait_sp(s["pack_zero"], 2)
                    wait_sp(s["pack_in"], u.count(PACK_LOADS * G, PACK_LOADS * g + PACK_LOADS // 2 * k))
                    hs = slice(g * HG, (g + 1) * HG)
                    for row, n, part, step in RUNS_OF_PARTS[k]:
                        src = dram[k][part:part + (n if step else 1), :, hs, :].rearrange("a d h q -> a d (h q)")
                        if not step:
                            src = src.to_broadcast([n, DH, HG * S])
                        sp.dma_start((Qp, Kp)[k][row * DH:(row + n) * DH, hs, :].rearrange("p h q -> p (h q)"), src)\
                            .then_inc(s["pack_in"], 16)
                if T - 2 in NM_AT:
                    g = NM_AT[T - 2]
                    wait_sp(s["a_m3"], u.count(4, g + 1))
                    wait_sp(s["pack_zero"], 2)
                    for part in range(3):
                        sp.dma_start(Qp[MAX_ROW + part:MAX_ROW + part + 1, g * HG:(g + 1) * HG, :],
                                     m_parts[:, part, :]).then_inc(s["a_m_in"], 16)
                if T == 119:
                    wait_sp(s["c_prTs"], u.count(1, 1))
                    wait_sp(s["y_gated"], u.count(8, 0))
                    sp.dma_start(gate_dram, gateT[:]).then_inc(s["gate_out"], 16)
                for e in range(E):
                    if T == (120 if e < GATE_RING else EXPERTS_AT + DOWN_LAG + 7 + 8 * (e - GATE_RING)):
                        if e == 0:
                            wait_sp(s["gate_out"], u.count(16, 16))
                            if i0 < 2:
                                sp.wait_ge(s["set_wl"], 2 * E)
                        if e >= GATE_RING:
                            wait_sp(s["y_gated"], u.count(8, e - GATE_RING + 1))
                        sp.dma_start(gate_b128[:, e % GATE_RING, :], gate_dram[e].partition_broadcast(128))\
                            .then_inc(s["gate_in"][e % GATE_RING], 16)
                if T == 18 - TICKS and i0 >= 0:
                    wait_sp(s["f_xT"], u.count(1, 0))
                    if i0 < MID_FIRST:
                        sp.dma_start(chunks(f_xn), rows_of(x, u.n % B)).then_inc(s["f_in"], 16)
                    else:
                        sp.wait_ge(s["ld_x"], 16)
                        wait_sp(s["m_stored"], (u.n - (B - 2)) * 16)
                        sp.dma_start(chunks(f_xn), rows_of(stream, u.n % B)).then_inc(s["f_in"], 16)
                if T == 180:
                    wait_sp(s["e_stored"], u.count(16, 0))
                    if i0 > MID_FIRST:
                        wait_sp(s["m_stored"], ended_mids(i, i0) * 16 + 16)
                    src = rows_of(x, u.n % B) if i0 < MID_FIRST else rows_of(stream, u.n % B)
                    sp.dma_start(chunks(resid), src).then_inc(s["e_in"], 16)
                if T == 191:
                    wait_sp(s["e_x"], u.count(1, 1))
                    sp.dma_start(rows_of(out, u.n % B), chunks(resid)).then_inc(s["e_stored"], 16)

            def ended_mids(i, i0):
                return i - MID_FIRST + 1 if i0 < MID_FIRST + B else B

            def mid(t, b, i, i0):
                if t == 0:
                    wait_sp(s["e_stored"], (b.n + 1) * 16)
                    wait_sp(s["m_out"], b.count(1, 0))
                    sp.dma_start(chunks(m_xn), rows_of(out, b.n % B)).then_inc(s["m_in"], 16)
                if t == 20:
                    wait_sp(s["e_stored"], (i - 2) * 16)
                    sp.dma_start(chunks(resid), rows_of(out, b.n % B)).then_inc(s["m_in2"], 16)
                if t == 33:
                    wait_sp(s["m_x"], b.count(1, 1))
                    sp.dma_start(rows_of(stream, b.n % B), chunks(resid)).then_inc(s["m_stored"], 16)

            sp.sem_inc(s["m_stored"], 16)
            run(sp, lambda i, p, i0: walk(i, p, i0, tick, mid))
            sp.wait_ge(s["e_stored"], 16 * UNITS)

        @block.gpsimd
        def _(pool):
            pool.memset(ident[:], 0.0).then_inc(s["ident0"], 1)
            pool.wait_ge(s["ident0"], 1)
            pool.affine_select(out=ident[:], in_=ident[:], compare_op=ALU.not_equal, fill=1.0, base=0,
                               pattern=[[-1, 128]], channel_multiplier=1).then_inc(s["ident_ready"], 1)
            pool.memset(minus_half[:], -0.5).then_inc(s["consts"], 1)
            pool.memset(eps_t[:], EPS).then_inc(s["consts"], 1)

            def load_expert(k):
                src = w1[k] if k < E else w2[k - E].rearrange("(f p) d -> p f d", p=128)
                dst, loaded, _ = staged(k)
                if k >= E:
                    dst = dst.rearrange("p (f d) -> p f d", f=FC)
                if k >= GATE_RING:
                    pool.wait_ge(s["set_wl"], k + 1 - GATE_RING)
                pool.dma_start(dst, src).then_inc(loaded, 16)

            def set_up():
                pool.memset(Kp[:].bitcast(F32), 0.0).then_inc(s["k_zero"], 1)
                pool.memset(Qp[:].bitcast(F32), 0.0).then_inc(s["pack_zero"], 1)
                for k in range(GATE_RING):
                    load_expert(k)
                pool.memset(heads8[:], 1.0).then_inc(s["heads0"], 1)
                pool.wait_ge(s["heads0"], 1)
                blocks = heads8[:].rearrange("p (h d) -> p h d", d=DH)
                pool.affine_select(out=blocks, in_=blocks, compare_op=ALU.is_ge, fill=0.0, base=0,
                                   pattern=[[-DH, H], [0, DH]], channel_multiplier=1).then_inc(s["heads1"], 1)
                pool.wait_ge(s["heads1"], 1)
                pool.affine_select(out=blocks, in_=blocks, compare_op=ALU.is_ge, fill=0.0, base=DH - 1,
                                   pattern=[[DH, H], [0, DH]], channel_multiplier=-1).then_inc(s["heads_ready"], 1)
                pool.wait_ge(s["ld_bc"], 16 * 6)
                pool.tensor_scalar(g2_b[:], g2_b[:], 0.5, None, ALU.mult).then_inc(s["g2_half"], 1)
                pool.tensor_scalar(b2_b[:], b2_b[:], 0.5, None, ALU.mult).then_inc(s["g2_half"], 1)

            def inv_std(key, n):
                _, mv, ve, rs = ln[key]
                wait(pool, s["consts"], 2)
                wait(pool, s[f"{key}_mv"], n + 1)
                pool.tensor_tensor(ve[:], mv[:, :, 1], eps_t[:], ALU.add).then_inc(s[f"{key}_ve"], 1)
                wait(pool, s[f"{key}_ve"], n + 1)
                pool.tensor_tensor(ve[:], ve[:], minus_half[:], ALU.pow).then_inc(s[f"{key}_rs"], 1)

            def tick(T, u, t, i, i0):
                if i0 == 0 and T == t and t % SPLIT_EVERY == 0:
                    k = t // SPLIT_EVERY
                    high, low = split_of(k)
                    pool.wait_ge(s["set_wh"], k + 1)
                    pool.tensor_tensor(low, staged(k)[0], high.bitcast(F32), ALU.subtract).then_inc(s["set_wl"], 1)
                if i0 == 0 and T == t and t % SPLIT_EVERY == 1 and t // SPLIT_EVERY + GATE_RING < 2 * E:
                    load_expert(t // SPLIT_EVERY + GATE_RING)
                if T == 22 - TICKS:
                    inv_std("f", u.n)
                    if i0 < 0:
                        set_up()
                for k, at in ((0, 39 - TICKS), (1, 42 - TICKS)):
                    if T == at:
                        wait(pool, s["f_p2"], u.count(2, k + 1))
                        pool.tensor_tensor(parts[k][:, 2, :], rest[:], parts[k][:, 1, :], ALU.subtract)\
                            .then_inc(s["f_p3"], 1)
                if T == 100:
                    inv_std("c", u.n)
                m = T - EXPERTS_AT - 1
                if 0 <= m < 64 and m % 2 == 0 and not alone(u, m // 2):
                    n = m // 2
                    wait(pool, s["h_hi"], u.count(32, n + 1))
                    wait(pool, s["y_mm"], u.count(32, n + 1 - RING))
                    pool.tensor_tensor(hidl[:, n % RING, :], hid[:, n % 2, :], hidh[:, n % RING, :].bitcast(F32),
                                       ALU.subtract).then_inc(s["h_lo"], 1)
                m = T - EXPERTS_AT - DOWN_LAG - 7
                if 0 <= m < 64 and m % 8 == 0:
                    e = m // 8
                    wait(pool, s["y_gated"], u.count(8, e + 1))
                    wait(pool, s["y_acc"], u.count(8, e))
                    ya = yacc[u.parity]
                    pool.tensor_tensor(ya[:], ya[:], gated[:], ALU.add).then_inc(s["y_acc"], 1)
                if T == 185:
                    inv_std("e", u.n)
                if T == 186:
                    wait(pool, s["e_in"], u.count(16, 16))
                    wait(pool, s["g2_half"], 2)
                    pool.tensor_tensor(chunks(resid), chunks(resid), b2_b[:].unsqueeze(1).to_broadcast([128, TC, D]),
                                       ALU.add).then_inc(s["e_zb"], 1)
                if T == 187 and i0 <= LAST_UNIT + 1:
                    end_block(pool, u)

            def mid(t, b, i, i0):
                if t == 3:
                    inv_std("m", b.n)
                if t == 32:
                    wait(pool, s["m_t"], b.count(1, 1))
                    wait(pool, s["m_in2"], b.count(16, 16))
                    pool.tensor_tensor(resid[:], resid[:], mq[:], ALU.add).then_inc(s["m_x"], 1)

            run(pool, lambda i, p, i0: walk(i, p, i0, tick, mid))

        @block.scalar
        def _(act):
            def set_up():
                act.wait_ge(s["set_cT"], 1)
                act.activation(cwh[:].rearrange("p j o -> p (j o)"), turned_conv[:, 0:3 * D], ACT.Copy)\
                    .then_inc(s["set_ch"], 1)
                act.wait_ge(s["set_qT"], 1)
                act.activation(qkh[:].rearrange("p j o -> p (j o)"), turned_qkv[:, 0:2 * D], ACT.Copy)\
                    .then_inc(s["set_qh"], 1)
                act.wait_ge(s["set_cols"], 1)

            def tick(T, u, t, i, i0):
                if i0 == 0 and T == t and t % SPLIT_EVERY == 0:
                    k = t // SPLIT_EVERY
                    src, loaded, value = staged(k)
                    act.wait_ge(loaded, value)
                    act.activation(split_of(k)[0], src, ACT.Copy).then_inc(s["set_wh"], 1)
                if T == 26 - TICKS:
                    wait(act, s["f_xT"], u.count(1, 1))
                    wait(act, s["f_conv"], u.count(1, 0))
                    if in_iteration(i0, "mid"):
                        wait(act, s["m_v"], i - MID_FIRST + 1)
                    wait(act, s["pads_zero"], 2)
                    act.activation(xh[:, 1:S + 1], misc[:], ACT.Copy).then_inc(s["f_xh"], 1)
                    if i0 < 0:
                        set_up()
                if T == 36 - TICKS:
                    wait(act, s["f_conv"], u.count(1, 1))
                    wait(act, s["f_qk"], u.count(2, 0))
                    act.activation(ch[:], misc[:], ACT.Identity, bias=col(V_CONV)).then_inc(s["f_ch"], 1)
                    wait(act, s["c_x1"], u.n - 1)
                    act.activation(conv[u.parity][:], misc[:], ACT.Identity, bias=col(V_CONV))\
                        .then_inc(s["f_c"], 1)
                for k, at, bias in ((0, 38 - TICKS, V_BQ), (1, 41 - TICKS, V_BK)):
                    if T == at:
                        wait(act, s["f_qk"], u.count(2, k + 1))
                        wait(act, s["parts_out"][k], u.count(48, 0))
                        act.activation(parts[k][:, 0, :], misc[:], ACT.Identity, bias=col(bias))\
                            .then_inc(s["f_p1"], 1)
                    if T == at + 1:
                        wait(act, s["f_r1"], u.count(2, k + 1))
                        act.activation(parts[k][:, 1, :], rest[:], ACT.Copy).then_inc(s["f_p2"], 1)
                        if i0 < 0 and k == 1:
                            act.wait_ge(s["ld_mid"], 48)
                            act.activation(mwh[:], mws, ACT.Copy).then_inc(s["set_mh"], 1)
                if T in NM_AT:
                    g = NM_AT[T]
                    wait(act, s["a_nmT"], u.count(4, g + 1))
                    wait(act, s["a_m_in"], u.count(48 * G, 48 * g))
                    act.activation(m_parts[:, 0, :], misc[0:HG * TC, 0:128], ACT.Copy).then_inc(s["a_m1"], 1)
                if T - 1 in NM_AT:
                    g = NM_AT[T - 1]
                    wait(act, s["a_r1"], u.count(4, g + 1))
                    act.activation(m_parts[:, 1, :], m_rest[:], ACT.Copy).then_inc(s["a_m2"], 1)
                if T - 42 in (0, 16, 32, 48):
                    g = (T - 42) // 16
                    wait(act, s["a_pv"], u.count(16, 4 * g + 4))
                    wait(act, s["a_ctxT"], u.count(4, g))
                    wait(act, s["c_x1"], u.n)
                    act.activation(ctxT[:], ctx_ps[:], ACT.Copy).then_inc(s["a_ctx"], 1)
                if P2_AT <= T < P2_AT + 64:
                    n, j = divmod(T - P2_AT, HG)
                    wait(act, s["a_s2"], u.count(64, T - P2_AT + 1))
                    wait(act, s["a_pv"], u.count(16, n - 1))
                    act.activation(probs[:, n % 2, j, :], score2[(T - P2_AT) % 2][:], ACT.Exp, scale=SCALE)\
                        .then_inc(s["a_exp"], 1)
                if T == 94:
                    wait(act, s["c_cT"], u.count(1, 1))
                    act.activation(ctxT[:], misc[:], ACT.Copy).then_inc(s["c_cTs"], 1)
                if T == 110:
                    wait(act, s["c_x1f"], u.count(1, 1))
                    wait(act, s["h_mm"], u.count(32, 0))
                    act.activation(x1h[:], misc[:], ACT.Identity, bias=col(V_B1), scale=col(V_G1))\
                        .then_inc(s["c_x1h"], 1)
                if T == 115:
                    wait(act, s["c_lg2"], u.count(1, 1))
                    act.activation(eg[:], lg2[:], ACT.Exp).then_inc(s["c_eg"], 1)
                if T == 118:
                    wait(act, s["c_prT"], u.count(1, 1))
                    wait(act, s["gate_out"], u.count(16, 0))
                    act.activation(gateT[:], misc[0:E, :], ACT.Copy).then_inc(s["c_prTs"], 1)
                m = T - EXPERTS_AT
                if 0 <= m < 64 and m % 2 == 0:
                    n = m // 2
                    wait(act, s["h_mm"], u.count(32, n + 1))
                    wait_lo(act, u, n - 1)
                    act.activation(hid[:, n % 2, :], hid_bank(u, n)[:], ACT.Relu, bias=col(n))\
                        .then_inc(s["h_full"], 1)
                if T == 183:
                    wait(act, s["e_T"], u.count(1, 1))
                    if i0 < UNITS + 1:
                        wait(act, s["c_xnT"], u.n + 2)
                    act.activation(zn[:], misc[:], ACT.Copy).then_inc(s["e_t"], 1)

            def mid(t, b, i, i0):
                if t == 8:
                    wait(act, s["m_xT"], b.count(1, 1))
                    wait(act, s["f_conv"], i + 1)
                    act.activation(mxh, misc[:], ACT.Copy).then_inc(s["m_xh"], 1)
                if t == 11:
                    wait(act, s["m_q"], b.count(1, 1))
                    act.activation(mq[:], misc[:], ACT.Identity, bias=col(V_MBQ)).then_inc(s["m_mq"], 1)
                if t == 21:
                    wait(act, s["m_sc"], b.count(1, 1))
                    act.activation(m_xn[:], m_xn[:], ACT.Exp, scale=SCALE).then_inc(s["m_ex"], 1)

            def iteration(i, p, i0):
                if i0 == 0:
                    act.wait_ge(s["set_oT"], 1)
                    act.wait_ge(s["set_ml"], 1)
                walk(i, p, i0, tick, mid)

            run(act, iteration)

        @block.vector
        def _(dve):
            for z in (xh, xl):
                dve.memset(z[:, 0:S + 2:S + 1].bitcast(F32), 0.0).then_inc(s["pads_zero"], 1)

            def set_up():
                dve.wait_ge(s["set_ch"], 1)
                dve.tensor_tensor(cwl[:].rearrange("p j o -> p (j o)"), turned_conv[:, 0:3 * D],
                                  cwh[:].bitcast(F32).rearrange("p j o -> p (j o)"), ALU.subtract)\
                    .then_inc(s["set_cl"], 1)
                dve.wait_ge(s["set_qh"], 1)
                dve.tensor_tensor(qkl[:].rearrange("p j o -> p (j o)"), turned_qkv[:, 0:2 * D],
                                  qkh[:].bitcast(F32).rearrange("p j o -> p (j o)"), ALU.subtract)
                dve.tensor_copy(wvT[:], turned_qkv[:, 2 * D:3 * D]).then_inc(s["set_ql"], 1)
                dve.wait_ge(s["set_vT"], 1)
                dve.tensor_copy(cols[:], turned_vec[:, 0:NV]).then_inc(s["set_cols"], 1)
                for p in range(2):
                    dve.memset(V[p][:], 1.0)
                dve.memset(ctx_ps[:], 0.0).then_inc(s["zero_v"], 1)
                dve.wait_ge(s["k_zero"], 1)
                dve.memset(Kp[MAX_ROW:MAX_ROW + 3].bitcast(F32), TWO_ONES).then_inc(s["pack_zero"], 1)

            def set_up_rest():
                dve.wait_ge(s["set_oT"], 1)
                dve.tensor_copy(woT[:], turned_wo[:, 0:D])
                dve.wait_ge(s["set_mh"], 1)
                dve.tensor_tensor(mwl[:], mws, mwh[:].bitcast(F32), ALU.subtract).then_inc(s["set_ml"], 1)
                dve.wait_ge(s["heads_ready"], 1)
                dve.tensor_reduce(dil_mask[:], heads8[:].rearrange("p (a r d) -> p r a d", r=DIL, d=DH), AX.XY,
                                  ALU.max).then_inc(s["mask_ready"], 1)
                dve.wait_ge(s["ld_bc"], 16 * 6)

            def moments(key, n, src):
                st, mv, _, _ = ln[key]
                for c in range(TC):
                    last = dve.bn_stats(st[:, c, :], src(c))
                last.then_inc(s[f"{key}_bn"], 1)
                wait(dve, s[f"{key}_bn"], n + 1)
                dve.sem_inc(s["held_dve"], 1)
                for c in range(TC):
                    last = dve.bn_aggr(mv[:, c, :], st[:, c, :])
                last.then_inc(s[f"{key}_mv"], 1)

            def normalise(key, n, dst, src, done):
                _, mv, rs, _ = ln[key]
                wait(dve, s[f"{key}_rs"], n + 1)
                for c in range(TC):
                    last = dve.tensor_scalar(chunk(dst, c), src(c), mv[:, c, 0:1], rs[:, c:c + 1],
                                             ALU.subtract, ALU.mult)
                last.then_inc(s[done], 1)

            def tick(T, u, t, i, i0):
                m = T - EXPERTS_AT - 1
                if 0 <= m < 64 and m % 2 == 0:
                    n = m // 2
                    wait(dve, s["h_full"], u.count(32, n + 1))
                    wait(dve, s["y_mm"], u.count(32, n + 1 - RING))
                    dve.tensor_copy(hidh[:, n % RING, :], hid[:, n % 2, :]).then_inc(s["h_hi"], 1)
                    if alone(u, n):
                        wait(dve, s["h_hi"], u.count(32, n + 1))
                        dve.tensor_tensor(hidl[:, n % RING, :], hid[:, n % 2, :],
                                          hidh[:, n % RING, :].bitcast(F32), ALU.subtract).then_inc(s["h_lo_alone"], 1)
                m = T - EXPERTS_AT - DOWN_LAG - 6
                if 0 <= m < 64 and m % 8 == 0:
                    e = m // 8
                    wait(dve, s["y_mm"], u.count(32, 4 * e + 4))
                    wait(dve, s["gate_in"][e % GATE_RING], u.count(32, 16 * (e // GATE_RING + 1)))
                    wait(dve, s["y_acc"], u.count(8, e))
                    dve.scalar_tensor_tensor(out=gated[:], in0=y_ps[:], scalar=col(V_B2 + e),
                                             in1=gate_b128[:, e % GATE_RING, :], op0=ALU.add, op1=ALU.mult)\
                        .then_inc(s["y_gated"], 1)
                if T == 184:
                    wait(dve, s["e_t"], u.count(1, 1))
                    moments("e", u.n, lambda c: chunk(zn, c))
                if T == 186:
                    normalise("e", u.n, zn, lambda c: chunk(zn, c), "e_zn")
                if T == 187 and i0 > LAST_UNIT + 1:
                    end_block(dve, u)
                if 0 <= T < 64:
                    h, qc = divmod(T, TC)
                    g = h // HG
                    wait(dve, s["a_s1"], u.count(64, T + 1))
                    if T % 16 == 0:
                        wait(dve, s["a_nmT"], u.count(4, g - 1))
                    dve.tensor_reduce(negmax[:, g % 2, T % 16:T % 16 + 1], score1[T % 2][:], AX.X, ALU.max,
                                      negate=True).then_inc(s["a_max"], 1)
                if T in NM_AT:
                    g = NM_AT[T]
                    wait(dve, s["a_m1"], u.count(4, g + 1))
                    dve.tensor_tensor(m_rest[:], misc[0:HG * TC, 0:128], m_parts[:, 0, :], ALU.subtract)\
                        .then_inc(s["a_r1"], 1)
                if T - 1 in NM_AT:
                    g = NM_AT[T - 1]
                    wait(dve, s["a_m2"], u.count(4, g + 1))
                    dve.tensor_tensor(m_parts[:, 2, :], m_rest[:], m_parts[:, 1, :], ALU.subtract)\
                        .then_inc(s["a_m3"], 1)
                if T in CTX_AT:
                    g = CTX_AT[T]
                    turned = misc[:].rearrange("p (c j r) -> p c j r", c=TC, j=HG)
                    wait(dve, s["a_ctxT"], u.count(4, g + 1))
                    wait(dve, s["c_cT"], u.count(1, 0))
                    dve.reciprocal(rden[:], turned[:, :, :, DH]).then_inc(s["a_rden"], 1)
                    wait(dve, s["a_rden"], u.count(4, g + 1))
                    dve.tensor_tensor(ctxs[:, :, g * HG:(g + 1) * HG, :], turned[:, :, :, 0:DH],
                                      rden[:].unsqueeze(3).to_broadcast([128, TC, HG, DH]), ALU.mult)\
                        .then_inc(s["a_norm"], 1)
                if T == 98:
                    wait(dve, s["c_x1"], u.count(1, 1))
                    wait(dve, s["e_x"], u.n - 1)
                    dve.tensor_tensor(x1n[:].rearrange("p (c d) -> p c d", c=TC),
                                      misc[:].rearrange("p (c d) -> p c d", c=TC),
                                      bo_b[:].unsqueeze(1).to_broadcast([128, TC, D]), ALU.add)\
                        .then_inc(s["c_x1p"], 1)
                if T == 99:
                    wait(dve, s["c_x1p"], u.count(1, 1))
                    moments("c", u.n, lambda c: chunk(x1n, c))
                if T == 102:
                    normalise("c", u.n, x1n, lambda c: chunk(x1n, c), "c_xn")
                if T == 110:
                    wait(dve, s["c_xnT"], u.count(1, 1))
                    wait(dve, s["e_T"], u.n - 1)
                    dve.tensor_scalar(yacc[u.parity][:], misc[:], col(V_G1), col(V_B1), ALU.mult, ALU.add)\
                        .then_inc(s["c_x1f"], 1)
                if T == 111:
                    wait(dve, s["c_x1h"], u.count(1, 1))
                    dve.tensor_tensor(x1l[:], yacc[u.parity][:], x1h[:].bitcast(F32), ALU.subtract)\
                        .then_inc(s["c_x1l"], 1)
                if T == 114:
                    wait(dve, s["c_gate"], u.count(1, 1))
                    dve.tensor_tensor(lg[:], misc[:, 0:TC * E].rearrange("p (c e) -> p c e", c=TC),
                                      gb_b[:].unsqueeze(1).to_broadcast([128, TC, E]), ALU.add)\
                        .then_inc(s["c_lg"], 1)
                    wait(dve, s["c_lg"], u.count(1, 1))
                    dve.tensor_reduce(gmax[:], lg[:], AX.X, ALU.max).then_inc(s["c_gmax"], 1)
                    wait(dve, s["c_gmax"], u.count(1, 1))
                    dve.tensor_tensor(lg2[:], lg[:], gmax[:].unsqueeze(2).to_broadcast([128, TC, E]),
                                      ALU.subtract).then_inc(s["c_lg2"], 1)
                if T == 116:
                    wait(dve, s["c_eg"], u.count(1, 1))
                    dve.tensor_reduce(gsum[:], eg[:], AX.X, ALU.add).then_inc(s["c_gsum"], 1)
                    wait(dve, s["c_gsum"], u.count(1, 1))
                    dve.reciprocal(ginv[:], gsum[:]).then_inc(s["c_ginv"], 1)
                    wait(dve, s["c_ginv"], u.count(1, 1))
                    dve.tensor_tensor(gate[u.parity][:], eg[:], ginv[:].unsqueeze(2).to_broadcast([128, TC, E]),
                                      ALU.mult).then_inc(s["c_pr"], 1)
                if T == 21 - TICKS:
                    wait(dve, s["f_in"], u.count(16, 16))
                    moments("f", u.n, lambda c: chunk(f_xn, c))
                if T == 24 - TICKS:
                    normalise("f", u.n, f_xn, lambda c: chunk(f_xn, c), "f_xn")
                if T == 26 - TICKS:
                    wait(dve, s["f_xh"], u.count(1, 1))
                    dve.tensor_tensor(xl[:, 1:S + 1], misc[:], xh[:, 1:S + 1].bitcast(F32), ALU.subtract)\
                        .then_inc(s["f_xl"], 1)
                    if i0 < 0:
                        set_up()
                if T == 36 - TICKS:
                    wait(dve, s["f_c"], u.count(1, 1))
                    dve.scalar_tensor_tensor(out=cl[:], in0=misc[:], scalar=col(V_CONV),
                                             in1=ch[:].bitcast(F32), op0=ALU.add, op1=ALU.subtract)\
                        .then_inc(s["f_cl"], 1)
                for k, at, bias in ((0, 38 - TICKS, V_BQ), (1, 41 - TICKS, V_BK)):
                    if T == at:
                        wait(dve, s["f_p1"], u.count(2, k + 1))
                        wait(dve, s["f_p3"], u.count(2, k))
                        dve.scalar_tensor_tensor(out=rest[:], in0=misc[:], scalar=col(bias),
                                                 in1=parts[k][:, 0, :], op0=ALU.add, op1=ALU.subtract)\
                            .then_inc(s["f_r1"], 1)
                        if i0 < 0 and k == 1:
                            set_up_rest()
                if T == 57 - TICKS:
                    wait(dve, s["f_v"], u.count(1, 1))
                    wait(dve, s["a_pv"], (u.n - 1) * 16)
                    dve.tensor_tensor(V[u.parity][:, :, :, 0:DH],
                                      misc[:].rearrange("p (c h d) -> p c h d", c=TC, h=H),
                                      bv_b[:].rearrange("p (h d) -> p h d", h=H).unsqueeze(1)
                                      .to_broadcast([128, TC, H, DH]), ALU.add).then_inc(s["f_vs"], 1)

            def by_offset(ap):
                return ap.rearrange("p (n s r) -> p n r s", n=NSG, r=DIL)

            def over_steps(v):
                return v[:].unsqueeze(3).to_broadcast([128, NSG, DIL, SEG // DIL])

            def mid(t, b, i, i0):
                if t == 2:
                    wait(dve, s["m_in"], b.count(16, 16))
                    moments("m", b.n, lambda c: chunk(m_xn, c))
                if t == 5:
                    normalise("m", b.n, m_xn, lambda c: chunk(m_xn, c), "m_xn")
                if t == 9:
                    wait(dve, s["m_xh"], b.count(1, 1))
                    dve.tensor_tensor(mxl, misc[:], mxh.bitcast(F32), ALU.subtract).then_inc(s["m_xl"], 1)
                if t == 14:
                    wait(dve, s["m_k"], b.count(1, 1))
                    wait(dve, s["m_mq"], b.count(1, 1))
                    dve.scalar_tensor_tensor(out=mq[:], in0=misc[:], scalar=col(V_MBK), in1=mq[:],
                                             op0=ALU.add, op1=ALU.mult).then_inc(s["m_qk"], 1)
                if t == 20:
                    wait(dve, s["m_s"], b.count(1, 1))
                    dve.tensor_reduce(mmax[:], by_offset(misc[:]), AX.X, ALU.max).then_inc(s["m_max"], 1)
                    wait(dve, s["m_max"], b.count(1, 1))
                    dve.tensor_tensor(by_offset(m_xn[:]), by_offset(misc[:]), over_steps(mmax), ALU.subtract)\
                        .then_inc(s["m_sc"], 1)
                if t == 22:
                    wait(dve, s["m_ex"], b.count(1, 1))
                    dve.tensor_reduce(msum[:], by_offset(m_xn[:]), AX.X, ALU.add).then_inc(s["m_sum"], 1)
                    wait(dve, s["m_sum"], b.count(1, 1))
                    dve.reciprocal(minv[:], msum[:]).then_inc(s["m_inv"], 1)
                    wait(dve, s["m_inv"], b.count(1, 1))
                    wait(dve, s["mask_ready"], 1)
                    dve.tensor_tensor(mwt[:], minv[:], dil_mask[:].unsqueeze(1).to_broadcast([128, NSG, DIL]),
                                      ALU.mult).then_inc(s["m_wt"], 1)
                if t == 23:
                    wait(dve, s["m_wt"], b.count(1, 1))
                    dve.tensor_tensor(by_offset(m_xn[:]), by_offset(m_xn[:]), over_steps(mwt), ALU.mult)\
                        .then_inc(s["m_w"], 1)
                if t == 24:
                    wait(dve, s["m_v"], b.count(1, 1))
                    wait(dve, s["m_w"], b.count(1, 1))
                    dve.scalar_tensor_tensor(out=m_xn[:], in0=misc[:], scalar=col(V_MBV), in1=m_xn[:],
                                             op0=ALU.add, op1=ALU.mult).then_inc(s["m_o"], 1)
                if t == 31:
                    wait(dve, s["m_out"], b.count(1, 1))
                    dve.tensor_tensor(mq[:].rearrange("p (c d) -> p c d", c=TC),
                                      misc[:].rearrange("p (c d) -> p c d", c=TC),
                                      mbo_b[:].unsqueeze(1).to_broadcast([128, TC, D]), ALU.add)\
                        .then_inc(s["m_t"], 1)

            run(dve, lambda i, p, i0: walk(i, p, i0, tick, mid))

        @block.tensor
        def _(pe):
            def three(dst, hi, lo, rhi, rlo, start=True, stop=True, before_rlo=None):
                pe.matmul(dst, hi, rhi, start=start, stop=False)
                pe.matmul(dst, lo, rhi, start=False, stop=False)
                if before_rlo:
                    wait(pe, *before_rlo)
                return pe.matmul(dst, hi, rlo, start=False, stop=stop)

            def set_up():
                pe.wait_ge(s["ld_conv"], 16)
                for j in range(3):
                    last = pe.transpose(turned_conv[:, j * D:(j + 1) * D], conv_raw[:, :, j], ident[:])
                last.then_inc(s["set_cT"], 1)
                pe.wait_ge(s["ld_qkv"], 16)
                for j in range(3):
                    last = pe.transpose(turned_qkv[:, j * D:(j + 1) * D], wqkv_raw[:, j, :], ident[:])
                last.then_inc(s["set_qT"], 1)
                pe.wait_ge(s["ld_vec"], 16 * 9)
                pe.transpose(turned_vec[:, 0:NV], vec_rows, ident[0:NV, 0:NV]).then_inc(s["set_vT"], 1)
                pe.wait_ge(s["ld_wo"], 16)
                pe.transpose(turned_wo[:, 0:D], wo_raw, ident[:]).then_inc(s["set_oT"], 1)
                pe.wait_ge(s["set_ql"], 1)

            pe.wait_ge(s["ident_ready"], 1)

            def tick(T, u, t, i, i0):
                p = u.parity
                if T == 26 - TICKS:
                    wait_misc(pe, t, i, i0)
                    wait(pe, s["f_xn"], u.count(1, 1))
                    for c in range(TC):
                        last = pe.transpose(chunk(misc, c), chunk(f_xn, c), ident[:])
                    last.then_inc(s["f_xT"], 1)
                    if i0 < 0:
                        set_up()
                if T == 36 - TICKS:
                    wait_misc(pe, t, i, i0)
                    wait(pe, s["f_xl"], u.count(1, 1))
                    for j in range(3):
                        last = three(misc[:], cwh[:, j, :], cwl[:, j, :], xh[:, j:j + S], xl[:, j:j + S],
                                     start=(j == 0), stop=(j == 2))
                    last.then_inc(s["f_conv"], 1)
                for k, at in ((0, 38 - TICKS), (1, 41 - TICKS)):
                    if T == at:
                        wait_misc(pe, t, i, i0)
                        wait(pe, s["f_cl"], u.count(1, 1))
                        three(misc[:], qkh[:, k, :], qkl[:, k, :], ch[:], cl[:]).then_inc(s["f_qk"], 1)
                if T == 57 - TICKS:
                    wait_misc(pe, t, i, i0)
                    wait(pe, s["f_c"], u.count(1, 1))
                    for c in range(TC):
                        last = pe.matmul(chunk(misc, c), chunk(conv[p], c), wvT[:], start=True, stop=True)
                    last.then_inc(s["f_v"], 1)
                    if i0 < 0:
                        pe.wait_ge(s["ld_small"], 32)
                if T in NM_AT:
                    g = NM_AT[T]
                    wait_misc(pe, t, i, i0)
                    wait(pe, s["a_max"], u.count(64, 16 * g + 16))
                    pe.transpose(misc[0:HG * TC, 0:128], negmax[:, g % 2, :], ident[:]).then_inc(s["a_nmT"], 1)
                if T in CTX_AT:
                    g = CTX_AT[T]
                    wait_misc(pe, t, i, i0)
                    wait(pe, s["a_ctx"], u.count(4, g + 1))
                    for c in range(TC):
                        last = pe.transpose(chunk(misc, c), chunk(ctxT, c), ident[:])
                    last.then_inc(s["a_ctxT"], 1)
                if T == 94:
                    wait_misc(pe, t, i, i0)
                    wait(pe, s["a_norm"], u.count(4, 4))
                    for c in range(TC):
                        last = pe.transpose(chunk(misc, c), ctxs[:, c, :, :].rearrange("p h d -> p (h d)"), ident[:])
                    last.then_inc(s["c_cT"], 1)
                if T == 98:
                    wait_misc(pe, t, i, i0)
                    wait(pe, s["c_cTs"], u.count(1, 1))
                    for c in range(TC):
                        pe.matmul(chunk(misc, c), chunk(ctxT, c), woT[:], start=True, stop=False)
                        last = pe.matmul(chunk(misc, c), chunk(conv[p], c), ident[:], start=False, stop=True)
                    last.then_inc(s["c_x1"], 1)
                if T == 114:
                    wait_misc(pe, t, i, i0)
                    for c in range(TC):
                        last = pe.matmul(misc[:, c * E:(c + 1) * E], chunk(yacc[p], c), gws[:], start=True, stop=True)
                    last.then_inc(s["c_gate"], 1)
                if T == 118:
                    wait_misc(pe, t, i, i0)
                    wait(pe, s["c_pr"], u.count(1, 1))
                    for c in range(TC):
                        last = pe.transpose(misc[0:E, c * 128:(c + 1) * 128], gate[p][:, c, :], ident[:])
                    last.then_inc(s["c_prT"], 1)
                if T == 183:
                    wait_misc(pe, t, i, i0)
                    wait(pe, s["y_acc"], u.count(8, 8))
                    for c in range(TC):
                        last = pe.transpose(chunk(misc, c), chunk(yacc[p], c), ident[:])
                    last.then_inc(s["e_T"], 1)
                if P2_AT <= T < P2_AT + 64:
                    k = T - P2_AT
                    n, j = divmod(k, HG)
                    g, kc = divmod(n, TC)
                    if k % 16 == 0:
                        wait(pe, s["a_m_in"], u.count(48 * G, 48 * (g + 1)))
                    wait(pe, s["a_exp"], u.count(64, k - 1))
                    pe.matmul(score2[k % 2][:], Kp[:, g * HG + j, kc * 128:(kc + 1) * 128],
                              Qp[:, g * HG + j, :], start=True, stop=True).then_inc(s["a_s2"], 1)
                if 0 <= T < 64:
                    h, qc = divmod(T, TC)
                    if T % 16 == 0:
                        wait(pe, s["pack_in"], u.count(PACK_LOADS * G, PACK_LOADS * (h // HG + 1)))
                    wait(pe, s["a_max"], u.count(64, T - 1))
                    pe.matmul(score1[T % 2][:], Qp[0:SCORE_ROWS, h, qc * 128:(qc + 1) * 128],
                              Kp[0:SCORE_ROWS, h, :], start=True, stop=True).then_inc(s["a_s1"], 1)
                k = T - P2_AT - PV_LAG
                if 0 <= k < 64 and k % HG == 0:
                    n = k // HG
                    g, kc = divmod(n, TC)
                    wait(pe, s["a_exp"], u.count(64, 4 * n + 4))
                    if n == 0:
                        wait(pe, s["f_vs"], u.count(1, 1))
                        wait(pe, s["zero_v"], 1)
                    if kc == 0:
                        wait(pe, s["a_ctx"], u.count(4, g))
                    for j in range(HG):
                        last = pe.matmul(ctx_ps[32 * j:32 * j + DH + 1, :], V[p][:, kc, g * HG + j, :],
                                         probs[:, n % 2, j, :], start=(kc == 0), stop=(kc == TC - 1))
                    last.then_inc(s["a_pv"], 1)
                m = T - EXPERTS_AT
                if 0 <= m < 64 and m % 2 == 0:
                    n = m // 2
                    if n == 0:
                        wait(pe, s["c_x1h"], u.count(1, 1))
                    if i0 < 2:
                        wait(pe, s["set_wl"], E)
                    wait(pe, s["h_full"], u.count(32, n - 1 if alone(u, n - 1) else n))
                    w = slice(n * 128, (n + 1) * 128)
                    three(hid_bank(u, n)[:], w1h[:, w], w1l[:, w], x1h[:], x1l[:],
                          before_rlo=(s["c_x1l"], u.count(1, 1)) if n == 0 else None).then_inc(s["h_mm"], 1)
                m = T - EXPERTS_AT - DOWN_LAG
                if 0 <= m < 64 and m % 2 == 0:
                    n = m // 2
                    e, f = divmod(n, FC)
                    wait_lo(pe, u, n + 1)
                    if f == 0:
                        wait(pe, s["y_gated"], u.count(8, e))
                        if i0 < 2:
                            wait(pe, s["set_wl"], 2 * E)
                    three(y_ps[:], w2h[:, n, :], w2l[:, n, :], hidh[:, n % RING, :], hidl[:, n % RING, :],
                          start=(f == 0), stop=(f == FC - 1)).then_inc(s["y_mm"], 1)

            def mid(t, b, i, i0):
                if t == 8:
                    wait_misc(pe, t, i, i0)
                    wait(pe, s["m_xn"], b.count(1, 1))
                    for c in range(TC):
                        last = pe.transpose(chunk(misc, c), chunk(m_xn, c), ident[:])
                    last.then_inc(s["m_xT"], 1)
                for k, at, done in ((0, 11, "m_q"), (1, 14, "m_k"), (2, 24, "m_v")):
                    if t == at:
                        wait_misc(pe, t, i, i0)
                        wait(pe, s["m_xl"], b.count(1, 1))
                        three(misc[:], mwh[:, k, :], mwl[:, k, :], mxh, mxl).then_inc(s[done], 1)
                if t == 20:
                    wait_misc(pe, t, i, i0)
                    wait(pe, s["m_qk"], b.count(1, 1))
                    pe.matmul(misc[:], heads8[:], mq[:], start=True, stop=True).then_inc(s["m_s"], 1)
                if t == 31:
                    wait_misc(pe, t, i, i0)
                    wait(pe, s["m_o"], b.count(1, 1))
                    for c in range(TC):
                        last = pe.matmul(chunk(misc, c), chunk(m_xn, c), mwo[:], start=True, stop=True)
                    last.then_inc(s["m_out"], 1)

            def first(T, u, t, i, i0):
                if T == 110:
                    wait_misc(pe, t, i, i0)
                    wait(pe, s["c_xn"], u.count(1, 1))
                    for c in range(TC):
                        last = pe.transpose(chunk(misc, c), chunk(x1n, c), ident[:])
                    last.then_inc(s["c_xnT"], 1)

            run(pe, lambda i, p, i0: walk(i, p, i0, tick, mid, first))


_INS = ["L0_attn_x", "L0_attn_Wq", "L0_attn_bq", "L0_attn_Wk", "L0_attn_bk", "L0_attn_Wv", "L0_attn_bv",
        "L0_attn_Wo", "L0_attn_bo", "L0_ffn_conv_w", "L0_ffn_conv_b", "L0_ffn_wqkv", "L0_ffn_bqkv", "L0_ffn_wo",
        "L0_ffn_bo", "L0_ffn_ln1_g", "L0_ffn_ln1_b", "L0_ffn_gate_w", "L0_ffn_gate_b", "L0_ffn_w1", "L0_ffn_b1",
        "L0_ffn_w2", "L0_ffn_b2", "L0_ffn_ln2_g", "L0_ffn_ln2_b"]


def kernel(**inputs):
    import concourse.bacc as bacc
    from concourse.bass_utils import run_bass_kernel_spmd

    nc = bacc.Bacc("TRN2", target_bir_lowering=False, num_devices=1)
    arrays, args = {}, []
    for name in _INS:
        a = np.ascontiguousarray(inputs[name])
        arrays[f"in_{name}"] = a
        args.append(nc.dram_tensor(f"in_{name}", a.shape, mybir.dt.from_np(a.dtype), kind="ExternalInput").ap())
    args.append(nc.dram_tensor("out", (B, S, D), F32, kind="ExternalOutput").ap())
    macaron(nc, *args)
    return run_bass_kernel_spmd(nc, [arrays], core_ids=[0]).results[0]["out"]
```
